# Optimizing a Trainium2 kernel written in Bass

```python
import numpy as np
import jax
import jax.numpy as jnp

def _softmax(x, axis=-1):
    return jax.nn.softmax(x, axis=axis)

def _gelu(x):
    return jax.nn.gelu(x, approximate=True)

def _silu(x):
    return jax.nn.silu(x)

def _sigmoid(x):
    return jax.nn.sigmoid(x)

def _layernorm(x, axis=-1, eps=1e-05):
    m = jnp.mean(x, axis=axis, keepdims=True)
    v = jnp.var(x, axis=axis, keepdims=True)
    return (x - m) / jnp.sqrt(v + eps)

def _scatter_add(tgt, idx, src, axis=0):
    return tgt.at[idx].add(src)

def _segment_sum(src, seg, n):
    return jax.ops.segment_sum(src, seg, n)
kernel_name = 'mk_decoder_postln_d1_seqx_r4_414bdd'

def setup_inputs(seed: int=0):
    np.random.seed(seed)
    _w = jnp.asarray

    def _rec_inputs():
        import jax
        import jax.numpy as jnp
        _rk = jax.random.key(seed)
        x = 7.22e-05 + 1 * jax.random.normal(jax.random.fold_in(_rk, 1), (64, 256, 256), jnp.float32)
        _lenS = 256 - jax.random.randint(jax.random.fold_in(_rk, 7), (64,), 0, max(1, 256 // 4) + 1, jnp.int32)
        _lenS2 = 120 - jax.random.randint(jax.random.fold_in(_rk, 8), (64,), 0, max(1, 120 // 4) + 1, jnp.int32)
        _ctx_1024P = jax.random.normal(jax.random.fold_in(_rk, 11), (64, 16, 256), jnp.float32)
        _ctx_1024c = jax.random.dirichlet(jax.random.fold_in(_rk, 511), 0.3 * jnp.ones((16,), jnp.float32), (64, 120))
        _ctx_1024t = jnp.einsum('bsk,bkd->bsd', _ctx_1024c, _ctx_1024P)
        _ctx_1024t = _ctx_1024t * jax.lax.rsqrt(jnp.mean(jnp.square(_ctx_1024t)) + 1e-12) * 0.953939
        ctx_1024 = 4.13588e-05 + 0.999923 * (_ctx_1024t + 0.3 * jax.random.normal(jax.random.fold_in(_rk, 611), (64, 120, 256), jnp.float32))
        return (x, ctx_1024)
    x, ctx_1024 = _rec_inputs()

    def _L0_attn_setup():
        import jax, jax.numpy as jnp
        import numpy as np
        HIDDEN = 256
        HEADS = 16
        HEAD_DIM = HIDDEN // HEADS
        BLOCK_SIZE = 64
        NUM_GLOBAL = 4
        SCALE = HEAD_DIM ** (-0.5)

        def _block_mask(seq_len):
            i = jnp.arange(seq_len)[:, None]
            j = jnp.arange(seq_len)[None, :]
            half = BLOCK_SIZE // 2
            window = jnp.abs(i - j) <= half
            glob = (i < NUM_GLOBAL) | (j < NUM_GLOBAL)
            return window | glob
        key = jax.random.key(seed)
        ks = jax.random.split(key, 9)
        B, S = (4, 512)
        x = jax.random.normal(ks[0], (B, S, HIDDEN), dtype=jnp.float32)
        std = HIDDEN ** (-0.5)
        Wq = jax.random.normal(ks[1], (HIDDEN, HIDDEN), dtype=jnp.float32) * std
        bq = jnp.zeros((HIDDEN,), jnp.float32)
        Wk = jax.random.normal(ks[2], (HIDDEN, HIDDEN), dtype=jnp.float32) * std
        bk = jnp.zeros((HIDDEN,), jnp.float32)
        Wv = jax.random.normal(ks[3], (HIDDEN, HIDDEN), dtype=jnp.float32) * std
        bv = jnp.zeros((HIDDEN,), jnp.float32)
        Wo = jax.random.normal(ks[4], (HIDDEN, HIDDEN), dtype=jnp.float32) * std
        bo = jnp.zeros((HIDDEN,), jnp.float32)
        return {'x': x, 'Wq': Wq, 'bq': bq, 'Wk': Wk, 'bk': bk, 'Wv': Wv, 'bv': bv, 'Wo': Wo, 'bo': bo}
    _L0_attn_all = _L0_attn_setup()
    _L0_attn_in = {k: v for k, v in _L0_attn_all.items() if k in ('Wq', 'bq', 'Wk', 'bk', 'Wv', 'bv', 'Wo', 'bo')}
    del _L0_attn_all

    def _L0_xattn_setup():
        import jax, jax.numpy as jnp
        import numpy as np
        B, SQ, SKV, E, H = (4, 512, 512, 256, 16)
        D = E // H
        key = jax.random.key(seed)
        ks = jax.random.split(key, 8)
        s = 1.0 / np.sqrt(D)
        return {'query': jax.random.normal(ks[0], (B, SQ, E), jnp.float32), 'key_value': jax.random.normal(ks[1], (B, SKV, E), jnp.float32), 'wq': jax.random.normal(ks[2], (H, D, D), jnp.float32) * s, 'bq': jnp.zeros((H, D), jnp.float32), 'wk': jax.random.normal(ks[3], (H, D, D), jnp.float32) * s, 'bk': jnp.zeros((H, D), jnp.float32), 'wv': jax.random.normal(ks[4], (H, D, D), jnp.float32) * s, 'bv': jnp.zeros((H, D), jnp.float32), 'wo': jax.random.normal(ks[5], (E, E), jnp.float32) * (1.0 / np.sqrt(E)), 'bo': jnp.zeros((E,), jnp.float32)}
    _L0_xattn_all = _L0_xattn_setup()
    _L0_xattn_in = {k: v for k, v in _L0_xattn_all.items() if k in ('wq', 'bq', 'wk', 'bk', 'wv', 'bv', 'wo', 'bo')}
    del _L0_xattn_all

    def _L0_ffn_setup():
        import jax, jax.numpy as jnp
        import numpy as np

        def _ste(w, w_q):
            return w + jax.lax.stop_gradient(w_q - w)

        def quantize_w8_per(w, axis):
            amax = jnp.clip(jnp.max(jnp.abs(w), axis=axis, keepdims=True), 1e-08, None)
            scale = 127.0 / amax
            w_q = jnp.clip(jnp.round(w * scale), -128.0, 127.0) / scale
            return _ste(w, w_q)

        def quantize_a16(x):
            amax = jnp.clip(jnp.max(jnp.abs(x)), 1e-08, None)
            scale = 32767.0 / amax
            x_q = jnp.clip(jnp.round(x * scale), -32768.0, 32767.0) / scale
            return _ste(x, x_q)
        key = jax.random.key(seed)
        k1, k2, k3 = jax.random.split(key, 3)
        d_model, d_ff = (256, 1024)
        x = jax.random.normal(k1, (4, 512, d_model), dtype=jnp.float32)
        W_in = jax.random.normal(k2, (d_model, d_ff), dtype=jnp.float32) / np.sqrt(d_model)
        b_in = jnp.zeros((d_ff,), dtype=jnp.float32)
        W_out = jax.random.normal(k3, (d_ff, d_model), dtype=jnp.float32) / np.sqrt(d_ff)
        b_out = jnp.zeros((d_model,), dtype=jnp.float32)
        return {'x': x, 'W_in': W_in, 'b_in': b_in, 'W_out': W_out, 'b_out': b_out}
    _L0_ffn_all = _L0_ffn_setup()
    _L0_ffn_in = {k: v for k, v in _L0_ffn_all.items() if k in ('W_in', 'b_in', 'W_out', 'b_out')}
    del _L0_ffn_all
    return {'x': x, 'ctx_1024': ctx_1024, 'L0_attn_Wq': _L0_attn_in['Wq'], 'L0_attn_bq': _L0_attn_in['bq'], 'L0_attn_Wk': _L0_attn_in['Wk'], 'L0_attn_bk': _L0_attn_in['bk'], 'L0_attn_Wv': _L0_attn_in['Wv'], 'L0_attn_bv': _L0_attn_in['bv'], 'L0_attn_Wo': _L0_attn_in['Wo'], 'L0_attn_bo': _L0_attn_in['bo'], 'L0_xattn_wq': _L0_xattn_in['wq'], 'L0_xattn_bq': _L0_xattn_in['bq'], 'L0_xattn_wk': _L0_xattn_in['wk'], 'L0_xattn_bk': _L0_xattn_in['bk'], 'L0_xattn_wv': _L0_xattn_in['wv'], 'L0_xattn_bv': _L0_xattn_in['bv'], 'L0_xattn_wo': _L0_xattn_in['wo'], 'L0_xattn_bo': _L0_xattn_in['bo'], 'L0_ffn_W_in': _L0_ffn_in['W_in'], 'L0_ffn_b_in': _L0_ffn_in['b_in'], 'L0_ffn_W_out': _L0_ffn_in['W_out'], 'L0_ffn_b_out': _L0_ffn_in['b_out']}

def reference(x, ctx_1024, L0_attn_Wq, L0_attn_bq, L0_attn_Wk, L0_attn_bk, L0_attn_Wv, L0_attn_bv, L0_attn_Wo, L0_attn_bo, L0_xattn_wq, L0_xattn_bq, L0_xattn_wk, L0_xattn_bk, L0_xattn_wv, L0_xattn_bv, L0_xattn_wo, L0_xattn_bo, L0_ffn_W_in, L0_ffn_b_in, L0_ffn_W_out, L0_ffn_b_out):
    import jax
    import jax.numpy as jnp

    def _L0_attn_ref(x, Wq, bq, Wk, bk, Wv, bv, Wo, bo):
        import jax, jax.numpy as jnp
        import numpy as np
        HIDDEN = 256
        HEADS = 16
        HEAD_DIM = HIDDEN // HEADS
        BLOCK_SIZE = 64
        NUM_GLOBAL = 4
        SCALE = HEAD_DIM ** (-0.5)

        def _block_mask(seq_len):
            i = jnp.arange(seq_len)[:, None]
            j = jnp.arange(seq_len)[None, :]
            half = BLOCK_SIZE // 2
            window = jnp.abs(i - j) <= half
            glob = (i < NUM_GLOBAL) | (j < NUM_GLOBAL)
            return window | glob
        B, S, _ = x.shape

        def proj(W, b):
            y = jnp.einsum('bsd,ed->bse', x, W) + b
            return y.reshape(B, S, HEADS, HEAD_DIM).transpose(0, 2, 1, 3)
        q = proj(Wq, bq)
        k = proj(Wk, bk)
        v = proj(Wv, bv)
        scores = jnp.einsum('bhsd,bhtd->bhst', q, k) * SCALE
        mask = _block_mask(S)
        scores = jnp.where(mask[None, None], scores, -jnp.inf)
        attn = jax.nn.softmax(scores, axis=-1)
        out = jnp.einsum('bhst,bhtd->bhsd', attn, v)
        out = out.transpose(0, 2, 1, 3).reshape(B, S, HIDDEN)
        return jnp.einsum('bsd,ed->bse', out, Wo) + bo

    def _L0_xattn_ref(query, key_value, wq, bq, wk, bk, wv, bv, wo, bo):
        import jax, jax.numpy as jnp
        import numpy as np
        B, SQ, SKV, E, H = (4, 512, 512, 256, 16)
        D = E // H
        b, sq, e = query.shape
        skv = key_value.shape[1]
        h, d = (wq.shape[0], wq.shape[1])
        q = query.reshape(b, sq, h, d)
        kv = key_value.reshape(b, skv, h, d)
        qh = jnp.einsum('bshd,hed->bshe', q, wq) + bq
        kh = jnp.einsum('bthd,hed->bthe', kv, wk) + bk
        vh = jnp.einsum('bthd,hed->bthe', kv, wv) + bv
        scores = jnp.einsum('bshd,bthd->bhst', qh, kh) / jnp.sqrt(jnp.asarray(d, qh.dtype))
        attn = jax.nn.softmax(scores, axis=-1)
        ctx = jnp.einsum('bhst,bthd->bshd', attn, vh)
        out = ctx.reshape(b, sq, e)
        return out @ wo.T + bo

    def _L0_ffn_ref(x, W_in, b_in, W_out, b_out):
        import jax, jax.numpy as jnp
        import numpy as np

        def _ste(w, w_q):
            return w + jax.lax.stop_gradient(w_q - w)

        def quantize_w8_per(w, axis):
            amax = jnp.clip(jnp.max(jnp.abs(w), axis=axis, keepdims=True), 1e-08, None)
            scale = 127.0 / amax
            w_q = jnp.clip(jnp.round(w * scale), -128.0, 127.0) / scale
            return _ste(w, w_q)

        def quantize_a16(x):
            amax = jnp.clip(jnp.max(jnp.abs(x)), 1e-08, None)
            scale = 32767.0 / amax
            x_q = jnp.clip(jnp.round(x * scale), -32768.0, 32767.0) / scale
            return _ste(x, x_q)
        W_in_sim = quantize_w8_per(W_in, axis=0)
        W_out_sim = quantize_w8_per(W_out, axis=1)
        x_sim = quantize_a16(x)
        hidden = jax.nn.gelu(x_sim @ W_in_sim + b_in, approximate=False)
        hidden_sim = quantize_a16(hidden)
        out = hidden_sim @ W_out_sim + b_out
        return out
    x = _layernorm(x + _L0_attn_ref(x, L0_attn_Wq, L0_attn_bq, L0_attn_Wk, L0_attn_bk, L0_attn_Wv, L0_attn_bv, L0_attn_Wo, L0_attn_bo), axis=-1)
    x = _layernorm(x + _L0_xattn_ref(x, ctx_1024, L0_xattn_wq, L0_xattn_bq, L0_xattn_wk, L0_xattn_bk, L0_xattn_wv, L0_xattn_bv, L0_xattn_wo, L0_xattn_bo), axis=-1)
    x = _layernorm(x + _L0_ffn_ref(x, L0_ffn_W_in, L0_ffn_b_in, L0_ffn_W_out, L0_ffn_b_out), axis=-1)
    return x

_drawn_inputs = setup_inputs


def setup_inputs(seed=0):
    import zlib

    import numpy as np

    out = dict(_drawn_inputs(seed))
    spreads = {'L0_attn_bq': (0.0, 0.496),
     'L0_attn_bk': (0.0, 0.8),
     'L0_attn_bv': (0.0, 0.1),
     'L0_attn_bo': (0.0, 0.1),
     'L0_xattn_bq': (0.0, 0.29),
     'L0_xattn_bk': (0.0, 0.8),
     'L0_xattn_bv': (0.0, 0.1),
     'L0_xattn_bo': (0.0, 0.1),
     'L0_ffn_b_in': (0.0, 0.1),
     'L0_ffn_b_out': (0.0, 0.1)}
    factors = {}
    for name, (base, spread) in spreads.items():
        noise = np.random.default_rng([zlib.crc32(name.encode()), seed]).standard_normal(out[name].shape)
        drawn = base * np.exp(spread * noise) if base else spread * noise
        out[name] = jnp.asarray(drawn.astype(out[name].dtype))
    for name, factor in factors.items():
        out[name] = (out[name] * factor).astype(out[name].dtype)
    return out
```

```python
from contextlib import ExitStack

import concourse.bass as bass
from concourse import mybir

F32 = mybir.dt.float32
BF16 = mybir.dt.bfloat16
I32 = mybir.dt.int32
ALU = mybir.AluOpType
ACT = mybir.ActivationFunctionType
AX = mybir.AxisListType

P = 128
LN_EPS = 1e-5
MASKED = -1e38
ROUND = 1.5 * 2.0 ** 23
NEWTON_STEPS = 3
NSLOT = 6
Q_SLOTS = ((0, 3), (3, 2), (5, 1))
K_SLOTS = ((0, 3, 5), (1, 4), (2,))


class Batch:

    def __init__(self, half, parity):
        self.half, self.parity = half, parity
        self.n = half * 2 + parity

    def count(self, per_batch, k):
        return self.n * per_batch + k


def wait(engine, semaphore, value):
    if isinstance(value, int) and value <= 0:
        return
    engine.wait_ge(semaphore, value)


def lone_wait(engine, passed, count, semaphore, value):
    if isinstance(value, int):
        wait(engine, semaphore, value)
        return
    value = engine.to_reg(engine.snap(value))
    engine.wait_ge(passed, count)
    engine.wait_ge(semaphore, value)


def run_steps(engine, n_batches, step):
    def at(b):
        return Batch(b // 2, b % 2) if 0 <= b < n_batches else None

    for s in range(-1, 3):
        step(at(s + 1), at(s), at(s - 1))
    with engine.Fori(0, (n_batches - 4) // 2) as i:
        step(Batch(i + 2, 0), Batch(i + 1, 1), Batch(i + 1, 0))
        step(Batch(i + 2, 1), Batch(i + 2, 0), Batch(i + 1, 1))
    for s in range(n_batches - 1, n_batches + 1):
        step(at(s + 1), at(s), at(s - 1))


class Attention:

    def __init__(self, cross, n_batches, s_q, s_kv, d, heads):
        self.cross, self.n, self.d, self.heads = cross, n_batches, d, heads
        self.dh = d // heads
        self.qt = s_q // P
        self.kt = 1 if cross else s_kv // P
        self.kp = s_kv // self.kt
        self.hpu = 2 // self.kt
        self.units = heads // self.hpu
        self.lag = 2
        self.upg = 4 // self.hpu
        self.ring = 4 if cross else 8
        self.kheads = 8 if cross else 4
        self.sides = ((P, 0, self.qt), (self.kp, self.qt, self.kt))
        if cross:
            self.pieces = [("q", 0), ("k", 0), ("s", 0), ("s", 1), ("q", 1), ("s", 2), ("s", 3),
                           ("q", 2), ("k", 1), ("s", 4), ("s", 5), ("q", 3), ("s", 6), ("s", 7)]
            self.first_piece = 1
        else:
            self.pieces = []
            for g in range(4):
                self.pieces += [("q", g), ("k", g)] + [("s", 4 * g + i) for i in range(4)]
            self.first_piece = 3

    def groups_at(self, j):
        g, rest = divmod(j - self.lag + 1, self.upg)
        return [g - 1] if rest == 0 and g >= 1 else []

    def pieces_at(self, j):
        k = 2 * (j - self.first_piece)
        return self.pieces[k:k + 2] if k >= 0 else []


def attention_layer(nc, a, x_in, ctx_in, weights, x_out, ident_f, ident_b, mask, cap, xres, x2max):
    wq, wk, wv, wo, bq, bk, bv, bo = weights
    d, heads, dh, qt, kt, kp = a.d, a.heads, a.dh, a.qt, a.kt, a.kp
    units, hpu = a.units, a.hpu
    sq = qt * P
    skv = kt * kp
    dk = d // P
    srows = NSLOT * dh
    nkst = heads // a.kheads
    dw = P if a.cross else d
    with ExitStack() as ctx:
        def sb(name, shape, dt=F32):
            return ctx.enter_context(nc.sbuf_tensor(f"{name}_{int(a.cross)}", shape, dt))

        def sem(name):
            return ctx.enter_context(nc.semaphore(f"{name}_{int(a.cross)}"))

        w_qkv = sb("w_qkv", [P, dk, 3, dw])
        w_o = sb("w_o", [P, dk, d])
        b_qkv = sb("b_qkv", [P, 3, d])
        b_o = sb("b_o", [P, d])
        xin = sb("xin", [P, qt, d])
        xres_in = [sb(f"xb{i}", [P, qt, d]) for i in range(2)]
        xT = sb("xT", [P, dk, sq])
        if a.cross:
            cin = sb("cin", [P, d])
            cT = sb("cT", [P, dk, skv])
        else:
            cT = xT
        qk32 = sb("qk32", [P, qt + kt, d])
        part1 = sb("part1", [P, qt + kt, d], BF16)
        part2 = sb("part2", [P, qt + kt, d], BF16)
        slots = sb("slots", [P, qt + kt, heads, srows], BF16)
        qst = [sb(f"qst{i}", [P, heads, sq], BF16) for i in range(2)]
        kst = [sb(f"kst{i}", [P, heads, skv], BF16) for i in range(2)]
        v = [sb(f"v{i}", [P, kt, heads, dh + 1]) for i in range(2)]
        negmax = sb("negmax", [P, heads, qt])
        if mask is not None:
            rowmax = sb("rowmax", [P, heads, qt])
        nm_rest = sb("nm_rest", [P, heads, qt])
        nm_parts = sb("nm_parts", [P, qt, 3, heads], BF16)
        nmT = sb("nmT", [3 * heads, sq], BF16)
        probs = [sb(f"probs{i}", [P, 512]) for i in range(a.ring)]
        rsum = sb("rsum", [P, qt, heads])
        o_raw = sb("o_raw", [P, heads // 4, sq])
        o_norm = o_raw[:].rearrange("p g q -> p (g q)")[:, 0:qt * d].rearrange("p (t e) -> p t e", e=d)
        oT = sb("oT", [P, dk, sq])
        stats = sb("stats", [P, qt, 6])
        mv = sb("mv", [P, qt, 2])
        var = sb("var", [P, qt])
        rstd0 = sb("rstd0", [P, qt])
        newton = sb("newton", [P, qt])
        rstd = sb("rstd", [P, qt])
        xo = [sb(f"xo{i}", [P, qt, d]) for i in range(2)]

        banks = [ctx.enter_context(nc.psum_tensor(f"bank{i}_{int(a.cross)}", [P, 512], F32)) for i in range(8)]
        f_bank, s_bank, e_bank, o_bank = banks[0:2], banks[2:4], banks[4:6], banks[6:8]

        ready = sem("constants_loaded")
        ones_set = sem("ones_set")
        x_loaded = [sem(f"x_loaded{i}") for i in range(2)]
        c_loaded = [sem(f"c_loaded{i}") for i in range(2)]
        nm_loaded = [sem(f"nm_loaded{i}") for i in range(2)]
        x_stored = [sem(f"x_stored{i}") for i in range(2)]
        front_done = sem("front_done")
        s_done = sem("s_done")
        st_done = sem("st_done")
        pv_done = sem("pv_done")
        ot_done = sem("ot_done")
        wo_done = sem("wo_done")
        x2t_done = sem("x2t_done")
        xT_ready = sem("xT_ready")
        cT_ready = sem("cT_ready")
        qk32_ready = sem("qk32_ready")
        v_ready = sem("v_ready")
        part1_ready = sem("part1_ready")
        rest1_ready = sem("rest1_ready")
        part2_ready = sem("part2_ready")
        part3_ready = sem("part3_ready")
        copies_ready = sem("copies_ready")
        qst_ready = sem("qst_ready")
        kst_ready = sem("kst_ready")
        s_read = sem("s_read")
        neg_ready = sem("neg_ready")
        masked = sem("masked")
        banks_set = sem("banks_set")
        raw_ready = sem("raw_ready")
        tok_done = sem("tok_done")
        nm_step = sem("nm_step")
        nmT_ready = sem("nmT_ready")
        probs_ready = sem("probs_ready")
        rsum_ready = sem("rsum_ready")
        o_ready = sem("o_ready")
        oT_ready = sem("oT_ready")
        resid_ready = sem("resid_ready")
        y_ready = sem("y_ready")
        stats_ready = sem("stats_ready")
        mv_ready = sem("mv_ready")
        var_ready = sem("var_ready")
        rstd0_ready = sem("rstd0_ready")
        newton_step = sem("newton_step")
        rstd_ready = sem("rstd_ready")
        xo_ready = sem("xo_ready")
        xmax_ready = sem("xmax_ready")
        x2T_ready = sem("x2T_ready")

        n_qk, n_v = 2, (1 if a.cross else 2)
        if a.cross:
            emptied = [(xT_ready, 1, 1), (cT_ready, 1, 1), (qk32_ready, 2, 1), (qk32_ready, 2, 2), (v_ready, 1, 1)]
        else:
            emptied = [(xT_ready, 1, 1), (qk32_ready, 2, 1), (qk32_ready, 2, 2), (v_ready, 2, 1), (v_ready, 2, 2)]
        filling = {}
        for kind, g in a.pieces:
            if kind == "q":
                filling["q", g] = len(emptied)
                emptied.append((qst_ready, 4, g + 1))
            elif kind == "k":
                filling["k", g] = len(emptied)
                emptied.append((kst_ready, nkst, g + 1))
        filling["nm"] = len(emptied)
        emptied.append((nmT_ready, 1, 1))
        n_front = len(emptied)
        assert n_front % 2 == 0

        n_const = 0
        x_view = x_in.rearrange("b (t p) d -> b p t d", p=P)
        xo_view = x_out.rearrange("b (t p) d -> b p t d", p=P)

        block = ctx.enter_context(nc.Block())

        n_w = 3 * (heads if a.cross else 1) + 1
        n_const = 16 * (n_w + 4)

        @block.sync
        def _(sp):
            if a.cross:
                sp.wait_ge(ones_set, 3)
                hk = heads // dk
                for i, w in enumerate((wq, wk, wv)):
                    for h in range(heads):
                        r = (h % hk) * dh
                        sp.dma_start(w_qkv[r:r + dh, h // hk, i, r:r + dh], w[h]).then_inc(ready, 16)
            else:
                for i, w in enumerate((wq, wk, wv)):
                    sp.dma_start(w_qkv[:, :, i, :], w.rearrange("(k p) e -> p k e", p=P)).then_inc(ready, 16)
            sp.dma_start(w_o[:], wo.rearrange("(k p) e -> p k e", p=P)).then_inc(ready, 16)
            for i, b in enumerate((bq, bk, bv)):
                sp.dma_start(b_qkv[:, i, :], b.partition_broadcast(P)).then_inc(ready, 16)
            sp.dma_start(b_o[:], bo.partition_broadcast(P)).then_inc(ready, 16)

            def load(b):
                lone_wait(sp, ready, n_const, resid_ready, b.count(1, 0))
                sp.dma_start(xin[:], x_view[b.n]).then_inc(x_loaded[b.parity], 16)
                if a.cross:
                    lone_wait(sp, ready, n_const, front_done, b.count(n_front, 2 - n_front))
                    sp.dma_start(cin[0:kp, :], ctx_in[b.n]).then_inc(c_loaded[b.parity], 16)

            def step(front, attend, end):
                if front is not None:
                    load(front)
                if end is not None:
                    lone_wait(sp, ready, n_const, xo_ready, end.count(2, 2))
                    sp.dma_start(xo_view[end.n], xo[end.parity][:]).then_inc(x_stored[end.parity], 16)
                if front is not None:
                    lone_wait(sp, ready, n_const, nmT_ready, front.count(1, 1))
                    lone_wait(sp, ready, n_const, st_done, front.count(units, -units))
                    for part in range(3):
                        sp.dma_start(qst[front.parity][srows + part:srows + part + 1, :, :],
                                     nmT[part * heads:(part + 1) * heads, :]).then_inc(nm_loaded[front.parity], 16)

            run_steps(sp, a.n, step)
            for i in range(2):
                sp.wait_ge(x_stored[i], 16 * (a.n // 2))

        @block.gpsimd
        def _(pool):
            for i in range(2):
                nc.gpsimd.memset(kst[i][srows:P, :, :], 1.0).then_inc(ones_set, 1)
                pool.wait_ge(ones_set, i + 1)
            if a.cross:
                nc.gpsimd.memset(w_qkv[:], 0.0).then_inc(ones_set, 1)
            for i in range(2):
                nc.gpsimd.memset(v[i][:, :, :, dh:dh + 1], 1.0).then_inc(ones_set, 1)
            pool.wait_ge(ones_set, 5 if a.cross else 4)
            ones = v[0][:, 0, 0, dh:dh + 1].unsqueeze(2).broadcast_to([P, qt, heads])
            pool.wait_ge(ready, n_const)

            def step(front, attend, end):
                if front is None:
                    return
                b = front
                pool.wait_ge(x_loaded[b.parity], (b.half + 1) * 16)
                wait(pool, y_ready, b.count(1, -1))
                pool.wait_ge(front_done, b.count(n_front, 1))
                nc.gpsimd.tensor_tensor(xres_in[b.parity][:], xin[:],
                                        b_o[:].unsqueeze(1).broadcast_to([P, qt, d]), ALU.add).then_inc(resid_ready, 1)
                for i, (rows, t0, n) in enumerate(a.sides):
                    pool.wait_ge(part1_ready, b.count(2, i + 1))
                    nc.gpsimd.tensor_tensor(qk32[0:rows, t0:t0 + n], qk32[0:rows, t0:t0 + n], part1[0:rows, t0:t0 + n],
                                            ALU.subtract).then_inc(rest1_ready, 1)
                for i, (rows, t0, n) in enumerate(a.sides):
                    pool.wait_ge(part2_ready, b.count(2, i + 1))
                    wait(pool, front_done, b.count(n_front, -1))
                    slot = Q_SLOTS[2][0] if i == 0 else K_SLOTS[2][0]
                    nc.gpsimd.tensor_tensor(
                        slots[0:rows, t0:t0 + n, :, slot * dh:(slot + 1) * dh],
                        qk32[0:rows, t0:t0 + n].rearrange("p t (h e) -> p t h e", e=dh),
                        part2[0:rows, t0:t0 + n].rearrange("p t (h e) -> p t h e", e=dh),
                        ALU.subtract).then_inc(part3_ready, 1)
                nm = negmax[:].rearrange("p h t -> p t h")
                rest = nm_rest[:].rearrange("p h t -> p t h")
                if mask is not None:
                    pool.wait_ge(neg_ready, b.count(1, 1))
                else:
                    pool.wait_ge(s_read, b.count(units, units))
                nc.gpsimd.tensor_tensor(nm_parts[:, :, 0, :], nm, ones, ALU.mult).then_inc(nm_step, 1)
                pool.wait_ge(nm_step, b.count(4, 1))
                nc.gpsimd.tensor_tensor(rest, nm, nm_parts[:, :, 0, :], ALU.subtract).then_inc(nm_step, 1)
                pool.wait_ge(nm_step, b.count(4, 2))
                nc.gpsimd.tensor_tensor(nm_parts[:, :, 1, :], rest, ones, ALU.mult).then_inc(nm_step, 1)
                pool.wait_ge(nm_step, b.count(4, 3))
                nc.gpsimd.tensor_tensor(nm_parts[:, :, 2, :], rest, nm_parts[:, :, 1, :], ALU.subtract).then_inc(nm_step, 1)

            run_steps(pool, a.n, step)

        @block.tensor
        def _(pe):
            pe.wait_ge(ready, n_const)
            pe.wait_ge(ones_set, 5 if a.cross else 4)
            pe.wait_ge(banks_set, 2)

            def fill(b, use):
                if use >= 2:
                    s, per, k = emptied[use - 2]
                    pe.wait_ge(s, b.count(per, k))
                else:
                    s, per, k = emptied[n_front - 2 + use]
                    wait(pe, s, b.count(per, k - per))
                return f_bank[use % 2]

            def front_start(b):
                bank = fill(b, 0)
                pe.wait_ge(x_loaded[b.parity], (b.half + 1) * 16)
                for k in range(dk):
                    for t in range(qt):
                        last = nc.tensor.transpose(bank[:, k * sq + t * P:k * sq + (t + 1) * P],
                                                   xin[:, t, k * P:(k + 1) * P], ident_f[:])
                last.then_inc(front_done, 1)
                if a.cross:
                    bank = fill(b, 1)
                    pe.wait_ge(c_loaded[b.parity], (b.half + 1) * 16)
                    for k in range(dk):
                        last = nc.tensor.transpose(bank[:, k * kp:(k + 1) * kp], cin[0:kp, k * P:(k + 1) * P],
                                                   ident_f[0:kp, 0:kp])
                    last.then_inc(front_done, 1)

            def project(b):
                pe.wait_ge(xT_ready, b.count(1, 1))
                if not a.cross:
                    for t in range(qt):
                        bank = fill(b, 1 + t)
                        for k in range(dk):
                            last = nc.tensor.matmul(bank[:], xT[:, k, t * P:(t + 1) * P],
                                                    w_qkv[:, k, 0:2, :], start=(k == 0), stop=(k == dk - 1))
                        last.then_inc(front_done, 1)
                    for t in range(qt):
                        bank = fill(b, 3 + t)
                        for k in range(dk):
                            last = nc.tensor.matmul(bank[:, 0:d], xT[:, k, t * P:(t + 1) * P],
                                                    w_qkv[:, k, 2, :], start=(k == 0), stop=(k == dk - 1))
                        last.then_inc(front_done, 1)
                    return
                bank = fill(b, 2)
                for t in range(qt):
                    for k in range(dk):
                        last = nc.tensor.matmul(bank[:, t * d + k * P:t * d + (k + 1) * P], xT[:, k, t * P:(t + 1) * P],
                                                w_qkv[:, k, 0, :], start=True, stop=True)
                last.then_inc(front_done, 1)
                pe.wait_ge(cT_ready, b.count(1, 1))
                for i in (1, 2):
                    bank = fill(b, 2 + i)
                    for k in range(dk):
                        last = nc.tensor.matmul(bank[0:kp, k * P:(k + 1) * P], cT[:, k, :],
                                                w_qkv[:, k, i, :], start=True, stop=True)
                    last.then_inc(front_done, 1)

            def stack(b, i, g):
                rows, t0, n = a.sides[i]
                hs = 4 if i == 0 else a.kheads
                bank = fill(b, filling["qk"[i], g])
                if g == 0:
                    pe.wait_ge(copies_ready, b.count(2, i + 1))
                    pe.wait_ge(part3_ready, b.count(2, i + 1))
                to = bank[:].bitcast(BF16)
                for h in range(hs):
                    for t in range(n):
                        at = (h * n + t) * rows
                        last = nc.tensor.transpose(to[0:srows, at:at + rows], slots[0:rows, t0 + t, g * hs + h, :],
                                                   ident_b[0:rows, 0:rows])
                last.then_inc(front_done, 1)

            def scores(b, u):
                wait(pe, s_read, b.count(units, u - 1))
                h0 = u * hpu
                pe.wait_ge(qst_ready, b.count(4, h0 // 4 + 1))
                pe.wait_ge(kst_ready, b.count(nkst, h0 // a.kheads + 1))
                bank = s_bank[u % 2]
                for h in range(h0, h0 + hpu):
                    for t in range(qt):
                        at = ((h - h0) * qt + t) * skv
                        last = nc.tensor.matmul(bank[:, at:at + skv], qst[b.parity][0:srows, h, t * P:(t + 1) * P],
                                                kst[b.parity][0:srows, h, :], start=True, stop=True)
                last.then_inc(s_done, 1)

            def scores_t(b, u):
                wait(pe, probs_ready, b.count(units, u - 1))
                if u == 0:
                    pe.wait_ge(nm_loaded[b.parity], (b.half + 1) * 48)
                bank = e_bank[u % 2]
                for i in range(2):
                    h, t = (u, i) if hpu == 1 else (u * hpu + i, 0)
                    last = nc.tensor.matmul(bank[0:kp, i * sq:(i + 1) * sq], kst[b.parity][0:srows + 3, h, t * kp:(t + 1) * kp],
                                            qst[b.parity][0:srows + 3, h, :], start=True, stop=True)
                last.then_inc(st_done, 1)

            def times_v(b, g):
                if g == 0:
                    wait(pe, x2T_ready if a.cross else oT_ready, b.count(1, 0))
                    pe.wait_ge(v_ready, b.count(n_v, n_v))
                if g == 2:
                    wait(pe, y_ready, b.count(1, 0))
                pe.wait_ge(masked if mask is not None else probs_ready, b.count(units, (g + 1) * a.upg))
                for k in range(kt):
                    for i in range(4):
                        h = 4 * g + i
                        u, half = h // hpu, (k if hpu == 1 else h % hpu)
                        last = nc.tensor.matmul(o_bank[g // 2][32 * i:32 * i + dh + 1, g % 2 * sq:(g % 2 + 1) * sq],
                                                v[b.parity][0:kp, k, h, :], probs[u % a.ring][0:kp, half * sq:(half + 1) * sq],
                                                start=(k == 0), stop=(k == kt - 1))
                last.then_inc(pv_done, 1)

            def step(front, attend, end):
                if end is not None:
                    pe.wait_ge(raw_ready, end.count(2, 2))
                    for t in range(qt):
                        for g in range(heads // 4):
                            last = nc.tensor.transpose(o_bank[t][:, g * P:(g + 1) * P], o_raw[:, g, t * P:(t + 1) * P], ident_f[:])
                    last.then_inc(tok_done, 1)
                if front is not None:
                    front_start(front)
                if end is not None:
                    pe.wait_ge(o_ready, end.count(2, 2))
                    for k in range(dk):
                        for t in range(qt):
                            last = nc.tensor.transpose(o_bank[0][:, k * sq + t * P:k * sq + (t + 1) * P],
                                                       o_norm[:, t, k * P:(k + 1) * P], ident_f[:])
                    last.then_inc(ot_done, 1)
                if front is not None:
                    project(front)
                if end is not None:
                    pe.wait_ge(oT_ready, end.count(1, 1))
                    for t in range(qt):
                        for k in range(dk):
                            last = nc.tensor.matmul(o_bank[1][:, t * d:(t + 1) * d], oT[:, k, t * P:(t + 1) * P],
                                                    w_o[:, k, :], start=(k == 0), stop=(k == dk - 1))
                    last.then_inc(wo_done, 1)
                for j in range(units):
                    if attend is not None:
                        scores_t(attend, j)
                    if end is not None and a.cross and j == 3:
                        pe.wait_ge(xo_ready, end.count(2, 2))
                        for k in range(dk):
                            for t in range(qt):
                                last = nc.tensor.transpose(o_bank[0][:, k * sq + t * P:k * sq + (t + 1) * P],
                                                           xo[end.parity][:, t, k * P:(k + 1) * P], ident_f[:])
                        last.then_inc(x2t_done, 1)
                    if attend is not None:
                        for g in a.groups_at(j):
                            times_v(attend, g)
                    if front is not None:
                        for kind, g in a.pieces_at(j):
                            if kind == "s":
                                scores(front, g)
                            else:
                                stack(front, "qk".index(kind), g)
                if attend is not None:
                    times_v(attend, heads // 4 - 1)
                if front is not None:
                    lone_wait(pe, ready, n_const, nm_step, front.count(4, 4))
                    bank = fill(front, filling["nm"])
                    for t in range(qt):
                        last = nc.tensor.transpose(bank[:].bitcast(BF16)[0:3 * heads, t * P:(t + 1) * P],
                                                   nm_parts[:, t, :, :].rearrange("p a h -> p (a h)"), ident_b[:])
                    last.then_inc(front_done, 1)

            run_steps(pe, a.n, step)

        @block.scalar
        def _(act):
            nc.scalar.preload_act_table_set("natural_log_exp_and_others")
            act.wait_ge(ready, n_const)

            def step(front, attend, end):
                b = front
                if end is not None:
                    act.wait_ge(pv_done, end.count(4, 4))
                    wait(act, ot_done, end.count(1, 0))
                    nc.scalar.activation(o_raw[:, 2:4, :].rearrange("p g q -> p (g q)"), o_bank[1][:], ACT.Copy).then_inc(raw_ready, 1)
                if b is not None:
                    act.wait_ge(front_done, b.count(n_front, 1))
                    wait(act, front_done, b.count(n_front, 5 - n_front))
                    nc.scalar.activation(xT[:].rearrange("p k q -> p (k q)"), f_bank[0][:], ACT.Copy).then_inc(xT_ready, 1)
                    if a.cross:
                        act.wait_ge(front_done, b.count(n_front, 2))
                        nc.scalar.activation(cT[:].rearrange("p k q -> p (k q)"), f_bank[1][:, 0:dk * kp],
                                             ACT.Copy).then_inc(cT_ready, 1)
                if end is not None:
                    act.wait_ge(ot_done, end.count(1, 1))
                    wait(act, wo_done, end.count(1, 0))
                    nc.scalar.activation(oT[:].rearrange("p k q -> p (k q)"), o_bank[0][:], ACT.Copy).then_inc(oT_ready, 1)
                if b is not None:
                    for i, (rows, t0, n) in enumerate(a.sides):
                        act.wait_ge(qk32_ready, b.count(2, i + 1 if a.cross else 2))
                        wait(act, copies_ready, b.count(2, i - 1))
                        nc.scalar.activation(part1[0:rows, t0:t0 + n], qk32[0:rows, t0:t0 + n], ACT.Copy).then_inc(part1_ready, 1)
                for j in range(units):
                    if attend is not None:
                        e = attend
                        act.wait_ge(st_done, e.count(units, j + 1))
                        wait(act, pv_done, e.count(4, (j - a.ring) // a.upg + 1))
                        nc.scalar.activation(probs[j % a.ring][0:kp, :], e_bank[j % 2][0:kp, :], ACT.Exp,
                                             scale=float(dh) ** -0.5).then_inc(probs_ready, 1)
                    if end is not None and j == 0:
                        act.wait_ge(var_ready, end.count(1, 1))
                        wait(act, rstd_ready, end.count(1, 0))
                        nc.scalar.activation(rstd0[:], var[:], ACT.Ln).then_inc(rstd0_ready, 1)
                        act.wait_ge(rstd0_ready, end.count(2, 1))
                        nc.scalar.activation(rstd0[:], rstd0[:], ACT.Exp, scale=-0.5).then_inc(rstd0_ready, 1)
                    if b is not None and j == a.first_piece - 1:
                        for i, (rows, t0, n) in enumerate(a.sides):
                            act.wait_ge(rest1_ready, b.count(2, i + 1))
                            wait(act, part3_ready, b.count(2, i - 1))
                            nc.scalar.activation(part2[0:rows, t0:t0 + n], qk32[0:rows, t0:t0 + n], ACT.Copy).then_inc(part2_ready, 1)
                    if end is not None and a.cross and j == 3:
                        act.wait_ge(x2t_done, end.count(1, 1))
                        nc.scalar.activation(xres[:, bass.ds(end.half, 1), :, end.parity * sq:(end.parity + 1) * sq],
                                             o_bank[0][:].rearrange("p (c k q) -> p c k q", c=1, k=dk), ACT.Copy).then_inc(x2T_ready, 1)
                    if b is not None:
                        for kind, g in a.pieces_at(j):
                            if kind == "k":
                                use = filling[kind, g]
                                act.wait_ge(front_done, b.count(n_front, use + 1))
                                wait(act, st_done, b.count(units, -units))
                                n = a.kheads * kt * kp
                                nc.scalar.activation(kst[b.parity][0:srows, g * a.kheads:(g + 1) * a.kheads, :],
                                                     f_bank[use % 2][:].bitcast(BF16)[0:srows, 0:n].rearrange("p (h k) -> p h k", k=skv),
                                                     ACT.Copy).then_inc(kst_ready, 1)
                if b is not None:
                    act.wait_ge(front_done, b.count(n_front, n_front))
                    wait(act, nm_loaded[1 - b.parity], (b.half + b.parity) * 48)
                    nc.scalar.activation(nmT[:], f_bank[1][:].bitcast(BF16)[0:3 * heads, 0:sq], ACT.Copy).then_inc(nmT_ready, 1)

            run_steps(act, a.n, step)

        @block.vector
        def _(dve):
            dve.wait_ge(ready, n_const)
            dve.wait_ge(ones_set, 5 if a.cross else 4)

            for i in range(2):
                nc.vector.memset(o_bank[i][:], 0.0).then_inc(banks_set, 1)

            def step(front, attend, end):
                b, o = front, end
                if o is not None:
                    dve.wait_ge(pv_done, o.count(4, 2))
                    wait(dve, ot_done, o.count(1, 0))
                    nc.vector.tensor_copy(o_raw[:, 0:2, :].rearrange("p g q -> p (g q)"), o_bank[0][:]).then_inc(raw_ready, 1)
                    for t in range(qt):
                        dve.wait_ge(tok_done, o.count(1, 1))
                        out = o_bank[t][:].rearrange("p (h e) -> p h e", e=32)
                        nc.vector.reciprocal(rsum[:, t, :], out[:, :, dh]).then_inc(rsum_ready, 1)
                    for t in range(qt):
                        dve.wait_ge(rsum_ready, o.count(2, t + 1))
                        out = o_bank[t][:].rearrange("p (h e) -> p h e", e=32)
                        nc.vector.tensor_tensor(o_norm[:, t, :].rearrange("p (h e) -> p h e", e=dh), out[:, :, 0:dh],
                                                rsum[:, t, :].unsqueeze(2).broadcast_to([P, heads, dh]),
                                                ALU.mult).then_inc(o_ready, 1)
                if b is not None:
                    if not a.cross:
                        for t in range(qt):
                            dve.wait_ge(front_done, b.count(n_front, 2 + t))
                            wait(dve, part3_ready, b.count(2, 0))
                            nc.vector.tensor_tensor(qk32[:].rearrange("p (i t) e -> p i t e", i=2)[:, :, t, :], f_bank[(1 + t) % 2][:].rearrange("p (i e) -> p i e", i=2),
                                                    b_qkv[:, 0:2, :], ALU.add).then_inc(qk32_ready, 1)
                    else:
                        for i, (rows, t0, n) in enumerate(a.sides):
                            dve.wait_ge(front_done, b.count(n_front, 3 + i))
                            wait(dve, part3_ready, b.count(2, 0))
                            nc.vector.tensor_tensor(qk32[0:rows, t0:t0 + n], f_bank[i][0:rows, 0:n * d].rearrange("p (t e) -> p t e", e=d),
                                                    b_qkv[0:rows, i, :].unsqueeze(1).broadcast_to([rows, n, d]),
                                                    ALU.add).then_inc(qk32_ready, 1)
                    wait(dve, pv_done, b.count(4, -4))
                    for t in range(kt):
                        use = (4 if a.cross else 3) + t
                        dve.wait_ge(front_done, b.count(n_front, use + 1))
                        nc.vector.tensor_tensor(v[b.parity][0:kp, t, :, 0:dh],
                                                f_bank[use % 2][0:kp, 0:d].rearrange("p (h e) -> p h e", e=dh),
                                                b_qkv[0:kp, 2, :].rearrange("p (h e) -> p h e", e=dh),
                                                ALU.add).then_inc(v_ready, 1)
                if o is not None:
                    dve.wait_ge(wo_done, o.count(1, 1))
                    dve.wait_ge(resid_ready, o.count(1, 1))
                    wait(dve, x_stored[o.parity], o.half * 16)
                    y = xo[o.parity]
                    nc.vector.tensor_tensor(y[:].rearrange("p t e -> p (t e)"), o_bank[1][:],
                                            xres_in[o.parity][:].rearrange("p t e -> p (t e)"), ALU.add).then_inc(y_ready, 1)
                    dve.wait_ge(y_ready, o.count(1, 1))
                    for t in range(qt):
                        nc.vector.bn_stats(stats[:, t, :], y[:, t, :]).then_inc(stats_ready, 1)
                    for t in range(qt):
                        lone_wait(dve, ready, n_const, stats_ready, o.count(2, t + 1))
                        nc.vector.bn_aggr(mv[:, t, :], stats[:, t, :]).then_inc(mv_ready, 1)
                    dve.wait_ge(mv_ready, o.count(2, 2))
                    nc.vector.tensor_scalar(var[:], mv[:, :, 1], LN_EPS, None, ALU.add).then_inc(var_ready, 1)
                if b is not None:
                    for i, (rows, t0, n) in enumerate(a.sides):
                        wait(dve, front_done, b.count(n_front, -1))
                        dve.wait_ge(part1_ready, b.count(2, i + 1))
                        one = part1[0:rows, t0:t0 + n].rearrange("p t (h e) -> p (t h) e", e=dh)
                        two = part2[0:rows, t0:t0 + n].rearrange("p t (h e) -> p (t h) e", e=dh)
                        to = slots[0:rows, t0:t0 + n].rearrange("p t h (s e) -> p (t h) s e", e=dh)
                        nh = n * heads
                        if i == 0:
                            nc.vector.tensor_copy(to[:, :, 0:3, :], one.unsqueeze(2).broadcast_to([rows, nh, 3, dh]))
                        else:
                            nc.vector.tensor_copy(to[:, :, 0:4:3, :], one.unsqueeze(2).broadcast_to([rows, nh, 2, dh]))
                            nc.vector.tensor_copy(to[:, :, 5, :], one)
                        dve.wait_ge(part2_ready, b.count(2, i + 1))
                        second = to[:, :, 3:5, :] if i == 0 else to[:, :, 1:5:3, :]
                        nc.vector.tensor_copy(second, two.unsqueeze(2).broadcast_to([rows, nh, 2, dh])).then_inc(copies_ready, 1)
                if o is not None:
                    y = xo[o.parity]
                    dve.wait_ge(rstd0_ready, o.count(2, 2))
                    nc.vector.tensor_tensor(newton[:], var[:], rstd0[:], ALU.mult).then_inc(newton_step, 1)
                    dve.wait_ge(newton_step, o.count(2, 1))
                    nc.vector.scalar_tensor_tensor(newton[:], newton[:], -0.5, rstd0[:], ALU.mult, ALU.mult).then_inc(newton_step, 1)
                    dve.wait_ge(newton_step, o.count(2, 2))
                    nc.vector.scalar_tensor_tensor(rstd[:], newton[:], 1.5, rstd0[:], ALU.add, ALU.mult).then_inc(rstd_ready, 1)
                    dve.wait_ge(rstd_ready, o.count(1, 1))
                    for t in range(qt):
                        nc.vector.tensor_scalar(xo[o.parity][:, t, :], y[:, t, :], mv[:, t, 0:1], rstd[:, t:t + 1],
                                                ALU.subtract, ALU.mult).then_inc(xo_ready, 1)
                    if a.cross:
                        dve.wait_ge(xo_ready, o.count(2, 2))
                        nc.vector.tensor_reduce(x2max[:, bass.ds(o.n, 1)], xo[o.parity][:].rearrange("p t e -> p (t e)"),
                                                AX.X, ALU.max, apply_absolute_value=True).then_inc(xmax_ready, 1)
                for j in range(units + 1):
                    if attend is not None and mask is not None and j > 0:
                        dve.wait_ge(probs_ready, attend.count(units, j))
                        nc.vector.tensor_tensor(probs[(j - 1) % a.ring][:], probs[(j - 1) % a.ring][:], cap[:],
                                                ALU.min).then_inc(masked, 1)
                    for kind, g in a.pieces_at(j) if b is not None else []:
                        if kind == "q":
                            use = filling[kind, g]
                            dve.wait_ge(front_done, b.count(n_front, use + 1))
                            wait(dve, st_done, b.count(units, -units))
                            nc.vector.tensor_copy(qst[b.parity][0:srows, g * 4:(g + 1) * 4, :],
                                                  f_bank[use % 2][:].bitcast(BF16)[0:srows, :].rearrange("p (h q) -> p h q", q=sq),
                                                  ).then_inc(qst_ready, 1)
                        elif kind == "s" and mask is None:
                            lone_wait(dve, ready, n_const, nm_step, b.count(4, 0))
                            dve.wait_ge(s_done, b.count(units, g + 1))
                            nc.vector.tensor_reduce(negmax[:, g * hpu:(g + 1) * hpu, :].rearrange("p h t -> p (h t)"),
                                                    s_bank[g % 2][:, 0:hpu * qt * skv].rearrange("p (a k) -> p a k", k=skv),
                                                    AX.X, ALU.max, negate=True).then_inc(s_read, 1)
                        elif kind == "s":
                            lone_wait(dve, ready, n_const, s_done, b.count(units, g + 1))
                            for t in range(qt):
                                sc = s_bank[g % 2][:, t * skv:(t + 1) * skv]
                                ins = nc.vector.tensor_tensor_reduce(out=sc, in0=sc, in1=mask[:, t * skv:(t + 1) * skv], scale=1.0,
                                                                     scalar=-3e38, op0=ALU.add, op1=ALU.max,
                                                                     accum_out=rowmax[:, g, t:t + 1])
                            ins.then_inc(s_read, 1)
                if b is not None and mask is not None:
                    dve.wait_ge(s_read, b.count(units, units))
                    wait(dve, nm_step, b.count(4, 0))
                    nc.vector.tensor_scalar(negmax[:], rowmax[:], -1.0, None, ALU.mult).then_inc(neg_ready, 1)

            run_steps(dve, a.n, step)


def decoder_layer(nc, x, ctx_in, attn, xattn, w_inT, b_in, w_out, b_out, out, x1, x2, stages=3):
    nb, s, d = x.shape
    heads = 16
    with ExitStack() as ctx:
        def sb(name, shape, dt=F32):
            return ctx.enter_context(nc.sbuf_tensor(name, shape, dt))

        ident_f = sb("ident_f", [P, P])
        ident_b = sb("ident_b", [P, P], BF16)
        x2max = sb("x2max", [P, nb])
        first = Attention(False, nb, s, s, d, heads)
        with ExitStack() as c2:
            mask = c2.enter_context(nc.sbuf_tensor("mask", [P, 2 * s], BF16))
            cap = c2.enter_context(nc.sbuf_tensor("cap", [P, 2 * s], BF16))
            made = c2.enter_context(nc.semaphore("made"))
            with nc.Block() as block:
                @block.gpsimd
                def _(pool):
                    half, n_global = 32, 4
                    n = [0]

                    def then(ins):
                        n[0] += 1
                        ins.then_inc(made, 1)
                        pool.wait_ge(made, n[0])

                    for m in (ident_f, ident_b):
                        then(nc.gpsimd.memset(m[:], 0.0))
                        then(nc.gpsimd.affine_select(out=m[:], in_=m[:], compare_op=ALU.not_equal, fill=1.0, base=0,
                                                     pattern=[[-1, P]], channel_multiplier=1))
                    for m, yes, no in ((mask, 0.0, MASKED), (cap, 3e38, 0.0)):
                        mk = m[:].rearrange("p (t k) -> p t k", t=2)
                        then(nc.gpsimd.memset(m[:], yes))
                        then(nc.gpsimd.affine_select(out=mk, in_=mk, compare_op=ALU.is_ge, fill=no, base=half,
                                                     pattern=[[P, 2], [-1, s]], channel_multiplier=1))
                        then(nc.gpsimd.affine_select(out=mk, in_=mk, compare_op=ALU.is_ge, fill=no, base=half,
                                                     pattern=[[-P, 2], [1, s]], channel_multiplier=-1))
                        then(nc.gpsimd.memset(mk[:, :, 0:n_global], yes))
                        then(nc.gpsimd.memset(mk[0:n_global, 0, :], yes))
            attention_layer(nc, first, x, None, attn, x1, ident_f, ident_b, mask, cap, None, None)
        xres = sb("xres", [P, nb // 2, d // P, 2 * s])
        second = Attention(True, nb, s, ctx_in.shape[1], d, heads)
        attention_layer(nc, second, x1, ctx_in, xattn, x2, ident_f, ident_b, None, None, xres, x2max)
        ffn_layer(nc, nb, s, d, ident_b, xres, x2max, w_inT, b_in, w_out, b_out, x2, out)


def ffn_layer(nc, nb, s, d, ident_b, xres, x2max, w_inT, b_in, w_out, b_out, x2, out):
    dff = w_inT.shape[0]
    dk, fj = d // P, dff // P
    tc = 512
    nchunk = nb * s // tc
    tt = tc // P
    npair = fj // 2
    with ExitStack() as ctx:
        def sb(name, shape, dt=F32):
            return ctx.enter_context(nc.sbuf_tensor(name, shape, dt))

        def sem(name):
            return ctx.enter_context(nc.semaphore(name))

        w1i = sb("w1i", [P, dk, dff], BF16)
        w2q = sb("w2q", [P, fj, d])
        b1 = sb("b1", [P, fj])
        b2 = sb("b2", [P, d])
        step1 = sb("step1", [P, fj])
        gain = sb("gain", [P, fj])
        amax = sb("amax", [P, 4])
        hmax = sb("hmax", [P, nchunk, npair])
        step2 = sb("step2", [P, fj])
        gather = sb("gather", [P, 4])

        banks = [ctx.enter_context(nc.psum_tensor(f"bank{i}_f", [P, 1024], F32)) for i in range(4)]
        loaded = sem("f_loaded")
        consts = sem("f_consts")
        prep = sem("f_prep")
        turned = sem("f_turned")
        kept = sem("f_kept")
        pooled = sem("f_pooled")

        with ExitStack() as c2:
            w1 = c2.enter_context(nc.sbuf_tensor("w1", [P, fj, d], F32))
            w1b = c2.enter_context(nc.sbuf_tensor("w1b", [P, fj, d], BF16))
            w2 = c2.enter_context(nc.sbuf_tensor("w2", [P, fj, d], F32))
            a1 = c2.enter_context(nc.sbuf_tensor("a1", [P, 2, fj], F32))
            sc = c2.enter_context(nc.sbuf_tensor("sc", [P, 2, fj], F32))
            with nc.Block() as block:
                @block.sync
                def _(sp):
                    sp.dma_start(w1[:], w_inT.rearrange("(j p) e -> p j e", p=P)).then_inc(loaded, 16)
                    sp.dma_start(w2[:], w_out.rearrange("(j p) e -> p j e", p=P)).then_inc(loaded, 16)
                    with nc.allow_non_contiguous_dma("a bias of 1024"):
                        sp.dma_start(b1[:], b_in.rearrange("(j p) -> p j", p=P)).then_inc(loaded, 16)
                    sp.dma_start(b2[:], b_out.partition_broadcast(P)).then_inc(loaded, 16)
                    sp.wait_ge(loaded, 64)

                @block.gpsimd
                def _(pool):
                    pool.wait_ge(prep, 1)
                    nc.gpsimd.partition_all_reduce(amax[:, 1:2], amax[:, 0:1], P, bass.bass_isa.ReduceOp.max).then_inc(pooled, 1)
                    pool.wait_ge(pooled, 1)

                @block.vector
                def _(dve):
                    n = [0]

                    def then(ins):
                        n[0] += 1
                        ins.then_inc(prep, 1)
                        dve.wait_ge(prep, n[0])

                    then(nc.vector.tensor_reduce(amax[:, 0:1], x2max[:], AX.X, ALU.max))
                    dve.wait_ge(loaded, 64)
                    for i, w in enumerate((w1, w2)):
                        then(nc.vector.tensor_reduce(a1[:, i, :], w[:], AX.X, ALU.max, apply_absolute_value=True))
                        then(nc.vector.tensor_scalar(a1[:, i, :], a1[:, i, :], 1e-8, None, ALU.max))
                        then(nc.vector.reciprocal(sc[:, i, :], a1[:, i, :]))
                        then(nc.vector.tensor_scalar(sc[:, i, :], sc[:, i, :], 127.0, None, ALU.mult))
                        for j in range(fj):
                            then(nc.vector.tensor_scalar(w[:, j, :], w[:, j, :], sc[:, i, j:j + 1], ROUND, ALU.mult, ALU.add))
                            then(nc.vector.tensor_scalar(w[:, j, :], w[:, j, :], ROUND, 127.0, ALU.subtract, ALU.min))
                        if i == 0:
                            then(nc.vector.tensor_scalar(w1b[:], w1[:], -128.0, None, ALU.max))
                            then(nc.vector.reciprocal(step1[:], sc[:, 0, :]))
                        else:
                            then(nc.vector.reciprocal(step2[:], sc[:, 1, :]))
                            for j in range(fj):
                                then(nc.vector.tensor_scalar(w2q[:, j, :], w2[:, j, :], -128.0, None, ALU.max))
                                then(nc.vector.tensor_scalar(w2q[:, j, :], w2q[:, j, :], step2[:, j:j + 1], None, ALU.mult))
                    dve.wait_ge(pooled, 1)
                    then(nc.vector.tensor_scalar(amax[:, 1:2], amax[:, 1:2], 1e-8, None, ALU.max))
                    then(nc.vector.reciprocal(amax[:, 2:3], amax[:, 1:2]))
                    then(nc.vector.tensor_scalar(amax[:, 2:3], amax[:, 2:3], 32767.0, None, ALU.mult))
                    then(nc.vector.reciprocal(amax[:, 3:4], amax[:, 2:3]))
                    then(nc.vector.tensor_scalar(gain[:], step1[:], amax[:, 3:4], None, ALU.mult))
                    for k in range(dk):
                        dve.wait_ge(turned, k + 1)
                        then(nc.vector.tensor_copy(w1i[:, k, :], banks[k][:].bitcast(BF16)[:, 0:dff]))

                @block.tensor
                def _(pe):
                    pe.wait_ge(prep, 1 + 4 + 2 * fj + 1)
                    for k in range(dk):
                        for j in range(fj):
                            last = nc.tensor.transpose(banks[k][:].bitcast(BF16)[:, j * P:(j + 1) * P],
                                                       w1b[:, j, k * P:(k + 1) * P], ident_b[:])
                        last.then_inc(turned, 1)

        xh = xres[:].bitcast(BF16).rearrange("p c k (two n) -> p c k two n", two=2)
        with ExitStack() as c2:
            t32 = c2.enter_context(nc.sbuf_tensor("t32", [P, dk, tc], F32))
            xi = [c2.enter_context(nc.sbuf_tensor(f"xi{i}", [P, dk, tc], F32)) for i in range(2)]
            hid = [c2.enter_context(nc.sbuf_tensor(f"hid{i}", [P, 2 * tc], F32)) for i in range(2)]
            shifted = c2.enter_context(nc.semaphore("shifted"))
            rounded = c2.enter_context(nc.semaphore("rounded"))
            high = c2.enter_context(nc.semaphore("high"))
            low = c2.enter_context(nc.semaphore("low"))
            h_done = c2.enter_context(nc.semaphore("h_done"))
            h_read = c2.enter_context(nc.semaphore("h_read"))
            g_read = c2.enter_context(nc.semaphore("g_read"))
            fin = c2.enter_context(nc.semaphore("fin"))

            def passes(engine, step):
                for c in range(2):
                    step(c, c)
                with engine.Fori(0, nchunk // 2 - 1) as i:
                    for c in range(2):
                        step(i * 2 + (2 + c), c)

            with nc.Block() as block:
                @block.vector
                def _(dve):
                    def quantize(c, p):
                        chunk = xres[:, bass.ds(c, 1), :, :]
                        wait(dve, rounded, c)
                        nc.vector.tensor_scalar(t32[:].unsqueeze(1), chunk, amax[:, 2:3], ROUND, ALU.mult, ALU.add).then_inc(shifted, 1)
                        dve.wait_ge(shifted, c + 1)
                        wait(dve, low, c - 1)
                        nc.vector.tensor_scalar(xi[p][:], t32[:], ROUND, 32767.0, ALU.subtract, ALU.min).then_inc(rounded, 1)

                    def step(c, p, ahead=True):
                        if ahead:
                            quantize(c + 1, 1 - p)
                        for j in range(npair):
                            dve.wait_ge(h_read, c * npair + (j + 1))
                            nc.vector.tensor_reduce(hmax[:, bass.ds(c, 1), j], hid[j % 2][:], AX.X, ALU.max,
                                                    apply_absolute_value=True).then_inc(g_read, 1)

                    quantize(0, 0)
                    step(0, 0)
                    step(1, 1)
                    with dve.Fori(0, nchunk // 2 - 2) as i:
                        step(i * 2 + 2, 0)
                        step(i * 2 + 3, 1)
                    step(nchunk - 2, 0)
                    step(nchunk - 1, 1, False)
                    dve.wait_ge(g_read, nchunk * npair)
                    nc.vector.tensor_reduce(gather[:, 0:1], hmax[:].rearrange("p c j -> p (c j)"), AX.X, ALU.max).then_inc(fin, 1)
                    dve.wait_ge(fin, 2)
                    nc.vector.tensor_scalar(gather[:, 1:2], gather[:, 1:2], 1e-8, None, ALU.max).then_inc(fin, 1)
                    dve.wait_ge(fin, 3)
                    nc.vector.reciprocal(gather[:, 2:3], gather[:, 1:2]).then_inc(fin, 1)
                    dve.wait_ge(fin, 4)
                    nc.vector.tensor_scalar(gather[:, 2:3], gather[:, 2:3], 32767.0, None, ALU.mult).then_inc(fin, 1)
                    dve.wait_ge(fin, 5)
                    nc.vector.reciprocal(gather[:, 3:4], gather[:, 2:3]).then_inc(fin, 1)
                    dve.wait_ge(fin, 6)

                @block.gpsimd
                def _(pool):
                    def step(c, p):
                        pool.wait_ge(high, c + 1)
                        nc.gpsimd.tensor_tensor(xh[:, bass.ds(c, 1), :, 1, :],
                                                xi[p][:].unsqueeze(1), xh[:, bass.ds(c, 1), :, 0, :], ALU.subtract).then_inc(low, 1)
                    passes(pool, step)
                    pool.wait_ge(fin, 1)
                    nc.gpsimd.partition_all_reduce(gather[:, 1:2], gather[:, 0:1], P, bass.bass_isa.ReduceOp.max).then_inc(fin, 1)

                @block.scalar
                def _(act):
                    def split(c, p):
                        act.wait_ge(rounded, c + 1)
                        nc.scalar.activation(xh[:, bass.ds(c, 1), :, 0, :], xi[p][:].unsqueeze(1), ACT.Copy).then_inc(high, 1)

                    def step(c, p, ahead=True):
                        for j in range(npair):
                            act.wait_ge(h_done, c * npair + (j + 1))
                            wait(act, g_read, c * npair + (j - 1))
                            for i in range(2):
                                ins = nc.scalar.activation(hid[j % 2][:, i * tc:(i + 1) * tc], banks[j][:, i * tc:(i + 1) * tc], ACT.Gelu,
                                                           bias=b1[:, 2 * j + i:2 * j + i + 1], scale=gain[:, 2 * j + i:2 * j + i + 1])
                            ins.then_inc(h_read, 1)
                            if j == 0 and ahead:
                                split(c + 1, 1 - p)

                    split(0, 0)
                    step(0, 0)
                    step(1, 1)
                    with act.Fori(0, nchunk // 2 - 2) as i:
                        step(i * 2 + 2, 0)
                        step(i * 2 + 3, 1)
                    step(nchunk - 2, 0)
                    step(nchunk - 1, 1, False)

                @block.tensor
                def _(pe):
                    def step(c, p):
                        pe.wait_ge(low, c + 1)
                        for j in range(npair):
                            wait(pe, h_read, c * npair + (j + 1 - npair))
                            for i in range(2):
                                col = (2 * j + i) * P
                                for k in range(dk):
                                    for part in range(2):
                                        last = nc.tensor.matmul(banks[j][:, i * tc:(i + 1) * tc], w1i[:, k, col:col + P],
                                                                xh[:, bass.ds(c, 1), k, part, :], start=(k + part == 0),
                                                                stop=(k == dk - 1 and part == 1))
                            last.then_inc(h_done, 1)
                    passes(pe, step)

        with ExitStack() as c2:
            def sb2(name, shape, dt=F32):
                return c2.enter_context(nc.sbuf_tensor(name, shape, dt))

            def sem2(name):
                return c2.enter_context(nc.semaphore(name))

            hid = [sb2(f"g{i}", [P, 2, tc]) for i in range(2)]
            h32 = [sb2(f"h32_{i}", [P, 2, tc]) for i in range(2)]
            hq = [sb2(f"hq{i}", [P, 2, tc]) for i in range(2)]
            xr = [sb2(f"xr{i}", [P, tt, d]) for i in range(2)]
            xb = [sb2(f"xrb{i}", [P, tt, d]) for i in range(2)]
            y = sb2("fy", [P, tt, d])
            stats = sb2("fstats", [P, tt, 6])
            mv = sb2("fmv", [P, tt, 2])
            rstd = sb2("frstd", [P, tt])
            var = sb2("fvar", [P, tt])
            bits = sb2("fbits", [P, tt], I32)
            newton = sb2("fnewton", [P, tt])
            xo = [sb2(f"fxo{i}", [P, tt, d]) for i in range(2)]
            h_done, h_read = sem2("h_done2"), sem2("h_read2")
            shifted, rounded = sem2("shifted2"), sem2("rounded2")
            o_done, y_ready = sem2("o_done"), sem2("y_ready2")
            used = sem2("hq_used")
            stats_ready, mv_ready, rstd_ready, xo_ready = sem2("st2"), sem2("mv2"), sem2("rstd2"), sem2("xo2")
            resid = sem2("resid2")
            x_loaded = [sem2(f"xl2_{i}") for i in range(2)]
            x_stored = [sem2(f"xs2_{i}") for i in range(2)]
            x_view = x2.rearrange("b (t p) d -> (b t) p d", p=P)
            o_view = out.rearrange("b (t p) d -> (b t) p d", p=P)

            def chunks(engine, step, tail=True):
                at = lambda c: Batch(c // 2, c % 2) if 0 <= c < nchunk else None
                for c in range(4):
                    step(at(c), at(c - 1))
                with engine.Fori(0, nchunk // 2 - 2) as i:
                    step(Batch(i + 2, 0), Batch(i + 1, 1))
                    step(Batch(i + 2, 1), Batch(i + 2, 0))
                step(None, at(nchunk - 1))

            with nc.Block() as block:
                @block.sync
                def _(sp):
                    def step(c, before):
                        if c is not None:
                            lone_wait(sp, loaded, 64, resid, c.count(1, -1))
                            sp.dma_start(xr[c.parity][:], x_view[bass.ds(c.n * tt, tt)].rearrange("t p d -> p t d")).then_inc(x_loaded[c.parity], 16)
                        if before is not None:
                            lone_wait(sp, loaded, 64, xo_ready, before.count(tt, tt))
                            sp.dma_start(o_view[bass.ds(before.n * tt, tt)].rearrange("t p d -> p t d"), xo[before.parity][:]).then_inc(x_stored[before.parity], 16)
                    chunks(sp, step)
                    for i in range(2):
                        sp.wait_ge(x_stored[i], 16 * (nchunk // 2))

                @block.gpsimd
                def _(pool):
                    def step(c, before):
                        if c is None:
                            return
                        pool.wait_ge(x_loaded[c.parity], (c.half + 1) * 16)
                        wait(pool, y_ready, c.count(tt, -tt))
                        nc.gpsimd.tensor_tensor(xb[c.parity][:], xr[c.parity][:], b2[:].unsqueeze(1).broadcast_to([P, tt, d]),
                                                ALU.add).then_inc(resid, 1)
                    chunks(pool, step)

                @block.tensor
                def _(pe):
                    def hidden(c, j):
                        wait(pe, h_read, c.count(npair, j - 1))
                        for i in range(2):
                            col = (2 * j + i) * P
                            for k in range(dk):
                                for part in range(2):
                                    last = nc.tensor.matmul(banks[j % 2][:, i * tc:(i + 1) * tc], w1i[:, k, col:col + P],
                                                            xh[:, bass.ds(c.n, 1), k, part, :], start=(k + part == 0),
                                                            stop=(k == dk - 1 and part == 1))
                        last.then_inc(h_done, 1)

                    def output(c, j):
                        if j == 0:
                            wait(pe, y_ready, c.count(tt, -tt))
                        pe.wait_ge(rounded, c.count(npair, j + 1))
                        for i in range(2):
                            for t in range(tt):
                                last = nc.tensor.matmul(banks[2 + c.parity][:, t * d:(t + 1) * d], hq[j % 2][:, i, t * P:(t + 1) * P],
                                                        w2q[:, 2 * j + i, :], start=(j + i == 0 and t % 2 == 0),
                                                        stop=(j == npair - 1 and i == 1), skip_group_check=True)
                        last.then_inc(used, 1)

                    def step(c, before):
                        for j in range(npair):
                            if c is not None:
                                hidden(c, j)
                            if j == 0 and before is not None:
                                output(before, npair - 1)
                            elif j > 0 and c is not None:
                                output(c, j - 1)
                    chunks(pe, step)

                @block.scalar
                def _(act):
                    def step(c, before):
                        if c is None:
                            return
                        for j in range(npair):
                            act.wait_ge(h_done, c.count(npair, j + 1))
                            wait(act, shifted, c.count(npair, j - 1))
                            for i in range(2):
                                ins = nc.scalar.activation(hid[j % 2][:, i, :], banks[j % 2][:, i * tc:(i + 1) * tc], ACT.Gelu,
                                                           bias=b1[:, 2 * j + i:2 * j + i + 1], scale=gain[:, 2 * j + i:2 * j + i + 1])
                            ins.then_inc(h_read, 1)
                    chunks(act, step)

                @block.vector
                def _(dve):
                    def finish(c):
                        dve.wait_ge(used, c.count(npair, npair))
                        dve.wait_ge(resid, c.count(1, 1))
                        for t in range(tt):
                            nc.vector.scalar_tensor_tensor(y[:, t, :], banks[2 + c.parity][:, t * d:(t + 1) * d], gather[:, 3:4],
                                                           xb[c.parity][:, t, :], ALU.mult, ALU.add).then_inc(y_ready, 1)
                        for t in range(tt):
                            dve.wait_ge(y_ready, c.count(tt, t + 1))
                            nc.vector.bn_stats(stats[:, t, :], y[:, t, :]).then_inc(stats_ready, 1)
                        for t in range(tt):
                            lone_wait(dve, loaded, 64, stats_ready, c.count(tt, t + 1))
                            nc.vector.bn_aggr(mv[:, t, :], stats[:, t, :]).then_inc(mv_ready, 1)
                        dve.wait_ge(mv_ready, c.count(tt, tt))
                        nstep = 3 + 3 * NEWTON_STEPS

                        def then(k, ins):
                            ins.then_inc(rstd_ready, 1)
                            dve.wait_ge(rstd_ready, c.count(nstep, k))

                        then(1, nc.vector.tensor_scalar(var[:], mv[:, :, 1], LN_EPS, None, ALU.add))
                        then(2, nc.vector.tensor_scalar(bits[:], var[:].bitcast(I32), 1, None, ALU.logical_shift_right))
                        then(3, nc.vector.tensor_scalar(rstd[:].bitcast(I32), bits[:], -1.0, float(0x5F3759DF), ALU.mult, ALU.add))
                        for k in range(NEWTON_STEPS):
                            then(4 + 3 * k, nc.vector.tensor_tensor(newton[:], var[:], rstd[:], ALU.mult))
                            then(5 + 3 * k, nc.vector.scalar_tensor_tensor(newton[:], newton[:], -0.5, rstd[:], ALU.mult, ALU.mult))
                            then(6 + 3 * k, nc.vector.scalar_tensor_tensor(rstd[:], newton[:], 1.5, rstd[:], ALU.add, ALU.mult))
                        wait(dve, x_stored[c.parity], c.half * 16)
                        for t in range(tt):
                            nc.vector.tensor_scalar(xo[c.parity][:, t, :], y[:, t, :], mv[:, t, 0:1], rstd[:, t:t + 1],
                                                    ALU.subtract, ALU.mult).then_inc(xo_ready, 1)

                    def step(c, before):
                        if c is not None:
                            for j in range(npair):
                                dve.wait_ge(h_read, c.count(npair, j + 1))
                                wait(dve, rounded, c.count(npair, j - 1))
                                nc.vector.tensor_scalar(h32[j % 2][:], hid[j % 2][:], gather[:, 2:3], ROUND, ALU.mult, ALU.add).then_inc(shifted, 1)
                                dve.wait_ge(shifted, c.count(npair, j + 1))
                                wait(dve, used, c.count(npair, j - 1))
                                nc.vector.tensor_scalar(hq[j % 2][:], h32[j % 2][:], ROUND, 32767.0, ALU.subtract, ALU.min).then_inc(rounded, 1)
                                if j == 1 and before is not None:
                                    finish(before)
                        elif before is not None:
                            finish(before)
                    chunks(dve, step)


_INS = ["x", "ctx_1024", "L0_attn_Wq", "L0_attn_bq", "L0_attn_Wk", "L0_attn_bk", "L0_attn_Wv", "L0_attn_bv",
        "L0_attn_Wo", "L0_attn_bo", "L0_xattn_wq", "L0_xattn_bq", "L0_xattn_wk", "L0_xattn_bk", "L0_xattn_wv",
        "L0_xattn_bv", "L0_xattn_wo", "L0_xattn_bo", "L0_ffn_W_in", "L0_ffn_b_in", "L0_ffn_W_out", "L0_ffn_b_out"]
_SWAPPED = {"L0_attn_Wq", "L0_attn_Wk", "L0_attn_Wv", "L0_attn_Wo", "L0_xattn_wq", "L0_xattn_wk", "L0_xattn_wv",
            "L0_xattn_wo", "L0_ffn_W_in"}
_FLAT = {"L0_xattn_bq", "L0_xattn_bk", "L0_xattn_bv"}


def kernel(**inputs):
    import numpy as np
    import concourse.bacc as bacc
    from concourse.bass_utils import run_bass_kernel_spmd

    nc = bacc.Bacc("TRN2", target_bir_lowering=False, num_devices=1)
    arrays, t = {}, {}
    for name in _INS:
        a = np.asarray(inputs[name])
        if name in _SWAPPED:
            a = np.swapaxes(a, -1, -2)
        if name in _FLAT:
            a = a.reshape(-1)
        a = np.ascontiguousarray(a)
        arrays[f"in_{name}"] = a
        t[name] = nc.dram_tensor(f"in_{name}", a.shape, mybir.dt.from_np(a.dtype), kind="ExternalInput").ap()
    shape = inputs["x"].shape
    out = nc.dram_tensor("out_0", shape, F32, kind="ExternalOutput").ap()
    x1 = nc.dram_tensor("x1_scratch", shape, F32, kind="Internal").ap()
    x2 = nc.dram_tensor("x2_scratch", shape, F32, kind="Internal").ap()
    attn = tuple(t[f"L0_attn_{n}"] for n in ("Wq", "Wk", "Wv", "Wo", "bq", "bk", "bv", "bo"))
    xattn = tuple(t[f"L0_xattn_{n}"] for n in ("wq", "wk", "wv", "wo", "bq", "bk", "bv", "bo"))
    decoder_layer(nc, t["x"], t["ctx_1024"], attn, xattn, t["L0_ffn_W_in"], t["L0_ffn_b_in"], t["L0_ffn_W_out"],
                  t["L0_ffn_b_out"], out, x1, x2)
    r = run_bass_kernel_spmd(nc, [arrays], core_ids=[0])
    return r.results[0]["out_0"]
```

```python
from contextlib import ExitStack

import concourse.bass as bass
from concourse import mybir

F32 = mybir.dt.float32
BF16 = mybir.dt.bfloat16
I32 = mybir.dt.int32
ALU = mybir.AluOpType
ACT = mybir.ActivationFunctionType
AX = mybir.AxisListType

P = 128
LN_EPS = 1e-5
MASKED = -1e38
ROUND = 1.5 * 2.0 ** 23
NEWTON_STEPS = 3
NSLOT = 6
Q_SLOTS = ((0, 3), (3, 2), (5, 1))
K_SLOTS = ((0, 3, 5), (1, 4), (2,))


class Batch:

    def __init__(self, half, parity):
        self.half, self.parity = half, parity
        self.n = half * 2 + parity

    def count(self, per_batch, k):
        return self.n * per_batch + k


def wait(engine, semaphore, value):
    if isinstance(value, int) and value <= 0:
        return
    engine.wait_ge(semaphore, value)


def lone_wait(engine, passed, count, *waits):
    waits = [(s, v if isinstance(v, int) else engine.to_reg(engine.snap(v))) for s, v in waits if s is not None]
    if not all(isinstance(v, int) for _, v in waits):
        engine.wait_ge(passed, count)
    for s, v in waits:
        wait(engine, s, v)


def run_steps(engine, n_batches, step):
    def at(b):
        return Batch(b // 2, b % 2) if 0 <= b < n_batches else None

    for s in range(-2, 3):
        step(at(s + 2), at(s + 1), at(s), at(s - 1))
    with engine.Fori(0, (n_batches - 6) // 2) as i:
        step(Batch(i + 2, 1), Batch(i + 2, 0), Batch(i + 1, 1), Batch(i + 1, 0))
        step(Batch(i + 3, 0), Batch(i + 2, 1), Batch(i + 2, 0), Batch(i + 1, 1))
    for s in range(n_batches - 3, n_batches + 1):
        step(at(s + 2), at(s + 1), at(s), at(s - 1))


SELF_PLAN = """q0 k0
s0 q1 tok
s1 k1 s2
ot s3 v
s4 wo q2
s5 k2
s6 x s7 y
s8 qk
s9 q3 ln s10
part1 k3 s11 xo
s12 s13 part2
s14
s15
neg
nm


"""
CROSS_PLAN = """q0 k0
tok s0 q1 s1
ot s2 v s3 k1 q2
wo s4 x s5
q3 y qk s6
s7 ln part1
neg xo part2
nm x2t

"""


class Attention:

    def __init__(self, cross, n_batches, s_q, s_kv, d, heads):
        self.cross, self.n, self.d, self.heads = cross, n_batches, d, heads
        self.dh = d // heads
        self.qt = s_q // P
        self.kt = 1 if cross else s_kv // P
        self.kp = s_kv // self.kt
        self.hpu = 2 // self.kt
        self.units = heads // self.hpu
        lag = 2
        self.upg = 4 // self.hpu
        self.ring = 4 if cross else 8
        self.kheads = 8 if cross else 4
        self.sides = ((P, 0, self.qt), (self.kp, self.qt, self.kt))
        self.plan = [("raw", 0)]
        for j, line in enumerate((CROSS_PLAN if cross else SELF_PLAN).split("\n")[:self.units + 1], -1):
            if j >= 0:
                self.plan.append(("e", j))
            g, rest = divmod(j - lag + 1, self.upg)
            if rest == 0 and g >= 1:
                self.plan.append(("pv", g - 1))
            for word in line.split():
                kind = word if word in ("x2t", "part1", "part2") else word.rstrip("0123456789")
                self.plan.append((kind, int(word[len(kind):] or 0)))
        self.plan.append(("pv", heads // 4 - 1))


def attention_layer(nc, a, x_in, ctx_in, weights, x_out, ident_f, ident_b, mask, xres, x2max):
    wq, wk, wv, wo, bq, bk, bv, bo = weights
    d, heads, dh, qt, kt, kp = a.d, a.heads, a.dh, a.qt, a.kt, a.kp
    units, hpu = a.units, a.hpu
    sq = qt * P
    skv = kt * kp
    dk = d // P
    srows = NSLOT * dh
    nkst = heads // a.kheads
    dw = P if a.cross else d
    with ExitStack() as ctx:
        def sb(name, shape, dt=F32):
            return ctx.enter_context(nc.sbuf_tensor(f"{name}_{int(a.cross)}", shape, dt))

        def sem(name):
            return ctx.enter_context(nc.semaphore(f"{name}_{int(a.cross)}"))

        w_qkv = sb("w_qkv", [P, dk, 3, dw])
        w_o = sb("w_o", [P, dk, d])
        b_qkv = sb("b_qkv", [P, 3, d])
        b_o = sb("b_o", [P, d])
        xin = sb("xin", [P, qt, d])
        xres_in = [sb(f"xb{i}", [P, qt, d]) for i in range(2)]
        xT = sb("xT", [P, dk, sq])
        if a.cross:
            cin = sb("cin", [P, d])
            cT = sb("cT", [P, dk, skv])
        else:
            cT = xT
        qk32 = sb("qk32", [P, qt + kt, d])
        part1 = sb("part1", [P, qt + kt, d], BF16)
        part2 = sb("part2", [P, qt + kt, d], BF16)
        slots = sb("slots", [P, qt + kt, heads, srows], BF16)
        qst = [sb(f"qst{i}", [P, heads, sq], BF16) for i in range(2)]
        kst = [sb(f"kst{i}", [P, heads, skv], BF16) for i in range(2)]
        v = [sb(f"v{i}", [P, kt, heads, dh + 1]) for i in range(2)]
        negmax = sb("negmax", [P, heads, qt])
        if mask is not None:
            rowmax = sb("rowmax", [P, heads, qt])
        nm_rest = sb("nm_rest", [P, heads, qt])
        nm_parts = sb("nm_parts", [P, qt, 3, heads], BF16)
        nmT = sb("nmT", [3 * heads, sq], BF16)
        probs = [sb(f"probs{i}", [P, 512]) for i in range(a.ring)]
        rsum = sb("rsum", [P, qt, heads])
        o_raw = sb("o_raw", [P, heads // 4, sq])
        o_norm = o_raw[:].rearrange("p g q -> p (g q)")[:, 0:qt * d].rearrange("p (t e) -> p t e", e=d)
        oT = sb("oT", [P, dk, sq])
        stats = sb("stats", [P, qt, 6])
        mv = sb("mv", [P, qt, 2])
        var = sb("var", [P, qt])
        rstd0 = sb("rstd0", [P, qt])
        newton = sb("newton", [P, qt])
        rstd = sb("rstd", [P, qt])
        xo = [sb(f"xo{i}", [P, qt, d]) for i in range(2)]

        banks = [ctx.enter_context(nc.psum_tensor(f"bank{i}_{int(a.cross)}", [P, 512], F32)) for i in range(8)]
        f_bank, s_bank, e_bank, o_bank = banks[0:2], banks[2:4], banks[4:6], banks[6:8]

        ready = sem("constants_loaded")
        ones_set = sem("ones_set")
        x_loaded = [sem(f"x_loaded{i}") for i in range(2)]
        c_loaded = [sem(f"c_loaded{i}") for i in range(2)]
        nm_loaded = [sem(f"nm_loaded{i}") for i in range(2)]
        x_stored = [sem(f"x_stored{i}") for i in range(2)]
        xb_loaded = [sem(f"xb_loaded{i}") for i in range(2)]
        early = sem("early_fillings")
        late = sem("late_fillings")
        s_done = sem("s_done")
        st_done = sem("st_done")
        pv_done = sem("pv_done")
        ot_done = sem("ot_done")
        wo_done = sem("wo_done")
        x2t_done = sem("x2t_done")
        xT_ready = sem("xT_ready")
        cT_ready = sem("cT_ready")
        qk32_ready = sem("qk32_ready")
        v_ready = sem("v_ready")
        part1_ready = sem("part1_ready")
        rest1_ready = sem("rest1_ready")
        part2_ready = sem("part2_ready")
        part3_ready = sem("part3_ready")
        copies_ready = sem("copies_ready")
        qst_ready = sem("qst_ready")
        kst_ready = sem("kst_ready")
        s_read = sem("s_read")
        neg_ready = sem("neg_ready")
        banks_set = sem("banks_set")
        raw_ready = sem("raw_ready")
        tok_done = sem("tok_done")
        nm_step = sem("nm_step")
        nmT_ready = sem("nmT_ready")
        probs_ready = sem("probs_ready")
        rsum_ready = sem("rsum_ready")
        o_ready = sem("o_ready")
        oT_ready = sem("oT_ready")
        resid_ready = sem("resid_ready")
        y_ready = sem("y_ready")
        stats_ready = sem("stats_ready")
        mv_ready = sem("mv_ready")
        var_ready = sem("var_ready")
        rstd0_ready = sem("rstd0_ready")
        newton_step = sem("newton_step")
        rstd_ready = sem("rstd_ready")
        xo_ready = sem("xo_ready")
        xmax_ready = sem("xmax_ready")
        x2T_ready = sem("x2T_ready")

        n_v = 1 if a.cross else 2
        fillings = []
        for kind, g in a.plan:
            if kind == "x":
                fillings.append(("x", xT_ready, 1, 1))
                if a.cross:
                    fillings.append(("c", cT_ready, 1, 1))
            elif kind == "qk":
                fillings += [("qk0", qk32_ready, 2, 1), ("qk1", qk32_ready, 2, 2)]
            elif kind == "v":
                fillings += [(f"v{t}", v_ready, n_v, t + 1) for t in range(n_v)]
            elif kind == "q":
                fillings.append((f"q{g}", qst_ready, 4, g + 1))
            elif kind == "k":
                fillings.append((f"k{g}", kst_ready, nkst, g + 1))
            elif kind == "nm":
                fillings.append(("nm", nmT_ready, 1, 1))
        names = [f[0] for f in fillings]
        is_early = [f[0] in ("x", "c", "qk0", "qk1") for f in fillings]
        n_early = sum(is_early)
        n_late = len(fillings) - n_early
        names_late = [name for name, first in zip(names, is_early) if not first]
        assert len(fillings) % 2 == 0

        def bank_of(name):
            return f_bank[names.index(name) % 2]

        def filled(b, name):
            i = names.index(name)
            if is_early[i]:
                return early, b.count(n_early, sum(is_early[:i + 1]))
            return late, b.count(n_late, i + 1 - sum(is_early[:i + 1]))

        x_view = x_in.rearrange("b (t p) d -> b p t d", p=P)
        xo_view = x_out.rearrange("b (t p) d -> b p t d", p=P)

        block = ctx.enter_context(nc.Block())

        hk = heads // dk
        n_w = 3 * (hk if a.cross else 1) + 1
        n_const = 16 * (n_w + 4)

        def load_blocks(engine, i):
            engine.wait_ge(ones_set, 3)
            blocks = (wq, wk, wv)[i].rearrange("(k h) p e -> h p k e", h=hk)
            for h in range(hk):
                rows = slice(h * dh, (h + 1) * dh)
                engine.dma_start(w_qkv[rows, :, i, rows], blocks[h]).then_inc(ready, 16)

        @block.sync
        def _(sp):
            if a.cross:
                load_blocks(sp, 0)
                load_blocks(sp, 2)
            else:
                for i, w in enumerate((wq, wk, wv)):
                    sp.dma_start(w_qkv[:, :, i, :], w.rearrange("(k p) e -> p k e", p=P)).then_inc(ready, 16)
            sp.dma_start(w_o[:], wo.rearrange("(k p) e -> p k e", p=P)).then_inc(ready, 16)
            for i, b in enumerate((bq, bk, bv)):
                sp.dma_start(b_qkv[:, i, :], b.partition_broadcast(P)).then_inc(ready, 16)
            sp.dma_start(b_o[:], bo.partition_broadcast(P)).then_inc(ready, 16)

            def step(new, front, attend, end):
                if new is not None:
                    b = new
                    lone_wait(sp, ready, n_const, (early, b.count(n_early, 1 - n_early)))
                    sp.dma_start(xin[:], x_view[b.n]).then_inc(x_loaded[b.parity], 16)
                    if a.cross:
                        lone_wait(sp, ready, n_const, (early, b.count(n_early, 2 - n_early)))
                        sp.dma_start(cin[0:kp, :], ctx_in[b.n]).then_inc(c_loaded[b.parity], 16)
                if attend is not None:
                    lone_wait(sp, ready, n_const, (y_ready, attend.count(1, -1)))
                    sp.dma_start(xres_in[attend.parity][:], x_view[attend.n]).then_inc(xb_loaded[attend.parity], 16)
                if end is not None:
                    lone_wait(sp, ready, n_const, (xo_ready, end.count(2, 2)))
                    sp.dma_start(xo_view[end.n], xo[end.parity][:]).then_inc(x_stored[end.parity], 16)
                if front is not None:
                    lone_wait(sp, ready, n_const, (nmT_ready, front.count(1, 1)))
                    lone_wait(sp, ready, n_const, (st_done, front.count(units, -units)))
                    for part in range(3):
                        sp.dma_start(qst[front.parity][srows + part:srows + part + 1, :, :],
                                     nmT[part * heads:(part + 1) * heads, :]).then_inc(nm_loaded[front.parity], 16)

            run_steps(sp, a.n, step)
            for i in range(2):
                sp.wait_ge(x_stored[i], 16 * (a.n // 2))

        @block.gpsimd
        def _(pool):
            for i in range(2):
                nc.gpsimd.memset(kst[i][srows:P, :, :], 1.0).then_inc(ones_set, 1)
                pool.wait_ge(ones_set, i + 1)
            if a.cross:
                nc.gpsimd.memset(w_qkv[:], 0.0).then_inc(ones_set, 1)
            for i in range(2):
                nc.gpsimd.memset(v[i][:, :, :, dh:dh + 1], 1.0).then_inc(ones_set, 1)
            pool.wait_ge(ones_set, 5 if a.cross else 4)
            ones = v[0][:, 0, 0, dh:dh + 1].unsqueeze(2).broadcast_to([P, qt, heads])
            pool.wait_ge(ready, n_const)

            def step(new, front, attend, end):
                for kind, g in a.plan:
                    if kind == "tok" and attend is not None:
                        b = attend
                        pool.wait_ge(xb_loaded[b.parity], (b.half + 1) * 16)
                        nc.gpsimd.tensor_tensor(xres_in[b.parity][:], xres_in[b.parity][:],
                                                b_o[:].unsqueeze(1).broadcast_to([P, qt, d]), ALU.add).then_inc(resid_ready, 1)
                    elif kind == "part1" and new is not None:
                        for i, (rows, t0, n) in enumerate(a.sides):
                            pool.wait_ge(part1_ready, new.count(2, i + 1))
                            nc.gpsimd.tensor_tensor(qk32[0:rows, t0:t0 + n], qk32[0:rows, t0:t0 + n],
                                                    part1[0:rows, t0:t0 + n], ALU.subtract).then_inc(rest1_ready, 1)
                    elif kind == "part2" and new is not None:
                        b = new
                        for i, (rows, t0, n) in enumerate(a.sides):
                            pool.wait_ge(part2_ready, b.count(2, i + 1))
                            wait(pool, late, b.count(n_late, -1))
                            slot = Q_SLOTS[2][0] if i == 0 else K_SLOTS[2][0]
                            nc.gpsimd.tensor_tensor(
                                slots[0:rows, t0:t0 + n, :, slot * dh:(slot + 1) * dh],
                                qk32[0:rows, t0:t0 + n].rearrange("p t (h e) -> p t h e", e=dh),
                                part2[0:rows, t0:t0 + n].rearrange("p t (h e) -> p t h e", e=dh),
                                ALU.subtract).then_inc(part3_ready, 1)
                    elif kind == "neg" and front is not None:
                        b = front
                        nm = negmax[:].rearrange("p h t -> p t h")
                        rest = nm_rest[:].rearrange("p h t -> p t h")
                        if mask is not None:
                            pool.wait_ge(neg_ready, b.count(1, 1))
                        else:
                            pool.wait_ge(s_read, b.count(units, units))
                        nc.gpsimd.tensor_tensor(nm_parts[:, :, 0, :], nm, ones, ALU.mult).then_inc(nm_step, 1)
                        pool.wait_ge(nm_step, b.count(4, 1))
                        nc.gpsimd.tensor_tensor(rest, nm, nm_parts[:, :, 0, :], ALU.subtract).then_inc(nm_step, 1)
                        pool.wait_ge(nm_step, b.count(4, 2))
                        nc.gpsimd.tensor_tensor(nm_parts[:, :, 1, :], rest, ones, ALU.mult).then_inc(nm_step, 1)
                        pool.wait_ge(nm_step, b.count(4, 3))
                        nc.gpsimd.tensor_tensor(nm_parts[:, :, 2, :], rest, nm_parts[:, :, 1, :], ALU.subtract).then_inc(nm_step, 1)

            run_steps(pool, a.n, step)

        @block.tensor
        def _(pe):
            pe.wait_ge(ready, n_const)
            pe.wait_ge(ones_set, 5 if a.cross else 4)
            pe.wait_ge(banks_set, 2)

            def emptied(b, name):
                i = names.index(name)
                late_n = b.n - 1 if is_early[i] else b.n
                for back in range(2, 2 * len(fillings) + 2, 2):
                    steps, at = divmod(i - back, len(fillings))
                    _, s, per, k = fillings[at]
                    n = late_n + steps + (1 if is_early[at] else 0)
                    if isinstance(n, int) and not 0 <= n < a.n:
                        continue
                    return s, n * per + k
                return None, 0

            def fill(b, name):
                s, value = emptied(b, name)
                if s is not None:
                    wait(pe, s, value)
                return bank_of(name)

            def turn(b):
                bank = fill(b, "x")
                pe.wait_ge(x_loaded[b.parity], (b.half + 1) * 16)
                for k in range(dk):
                    for t in range(qt):
                        last = nc.tensor.transpose(bank[:, k * sq + t * P:k * sq + (t + 1) * P],
                                                   xin[:, t, k * P:(k + 1) * P], ident_f[:])
                last.then_inc(early, 1)
                if a.cross:
                    bank = fill(b, "c")
                    pe.wait_ge(c_loaded[b.parity], (b.half + 1) * 16)
                    for k in range(dk):
                        last = nc.tensor.transpose(bank[:, k * kp:(k + 1) * kp], cin[0:kp, k * P:(k + 1) * P],
                                                   ident_f[0:kp, 0:kp])
                    last.then_inc(early, 1)

            def project_qk(b):
                pe.wait_ge(xT_ready, b.count(1, 1))
                if not a.cross:
                    for t in range(qt):
                        bank = fill(b, f"qk{t}")
                        for k in range(dk):
                            last = nc.tensor.matmul(bank[:], xT[:, k, t * P:(t + 1) * P],
                                                    w_qkv[:, k, 0:2, :], start=(k == 0), stop=(k == dk - 1))
                        last.then_inc(early, 1)
                    return
                bank = fill(b, "qk0")
                for t in range(qt):
                    for k in range(dk):
                        last = nc.tensor.matmul(bank[:, t * d + k * P:t * d + (k + 1) * P], xT[:, k, t * P:(t + 1) * P],
                                                w_qkv[:, k, 0, :], start=True, stop=True)
                last.then_inc(early, 1)
                pe.wait_ge(cT_ready, b.count(1, 1))
                bank = fill(b, "qk1")
                for k in range(dk):
                    last = nc.tensor.matmul(bank[0:kp, k * P:(k + 1) * P], cT[:, k, :],
                                            w_qkv[:, k, 1, :], start=True, stop=True)
                last.then_inc(early, 1)

            def project_v(b):
                for t in range(kt):
                    bank = fill(b, f"v{t}")
                    for k in range(dk):
                        if a.cross:
                            last = nc.tensor.matmul(bank[0:kp, k * P:(k + 1) * P], cT[:, k, :],
                                                    w_qkv[:, k, 2, :], start=True, stop=True)
                        else:
                            last = nc.tensor.matmul(bank[:, 0:d], xT[:, k, t * P:(t + 1) * P],
                                                    w_qkv[:, k, 2, :], start=(k == 0), stop=(k == dk - 1))
                    last.then_inc(late, 1)

            def stack(b, i, g):
                rows, t0, n = a.sides[i]
                hs = 4 if i == 0 else a.kheads
                bank = fill(b, f"{'qk'[i]}{g}")
                if g == 0:
                    pe.wait_ge(copies_ready, b.count(4, i + 3))
                    pe.wait_ge(part3_ready, b.count(2, i + 1))
                to = bank[:].bitcast(BF16)
                for h in range(hs):
                    for t in range(n):
                        at = (h * n + t) * rows
                        last = nc.tensor.transpose(to[0:srows, at:at + rows], slots[0:rows, t0 + t, g * hs + h, :],
                                                   ident_b[0:rows, 0:rows])
                last.then_inc(late, 1)

            def scores(b, u):
                wait(pe, s_read, b.count(units, u - 1))
                h0 = u * hpu
                pe.wait_ge(qst_ready, b.count(4, h0 // 4 + 1))
                pe.wait_ge(kst_ready, b.count(nkst, h0 // a.kheads + 1))
                bank = s_bank[u % 2]
                for h in range(h0, h0 + hpu):
                    for t in range(qt):
                        at = ((h - h0) * qt + t) * skv
                        last = nc.tensor.matmul(bank[:, at:at + skv], qst[b.parity][0:srows, h, t * P:(t + 1) * P],
                                                kst[b.parity][0:srows, h, :], start=True, stop=True)
                last.then_inc(s_done, 1)

            def scores_t(b, u):
                wait(pe, probs_ready, b.count(units, u - 1))
                if u == 0:
                    pe.wait_ge(nm_loaded[b.parity], (b.half + 1) * 48)
                bank = e_bank[u % 2]
                if mask is not None:
                    nc.tensor.matmul(bank[:], ident_b[:], mask[:], start=True, stop=False, skip_group_check=True)
                for i in range(2):
                    h, t = (u, i) if hpu == 1 else (u * hpu + i, 0)
                    last = nc.tensor.matmul(bank[0:kp, i * sq:(i + 1) * sq], kst[b.parity][0:srows + 3, h, t * kp:(t + 1) * kp],
                                            qst[b.parity][0:srows + 3, h, :], start=mask is None, stop=True, skip_group_check=True)
                last.then_inc(st_done, 1)

            def times_v(b, g):
                if g == 0:
                    wait(pe, oT_ready, b.count(1, 0))
                    pe.wait_ge(v_ready, b.count(n_v, n_v))
                if g == 2:
                    wait(pe, x2T_ready if a.cross else y_ready, b.count(1, 0))
                pe.wait_ge(probs_ready, b.count(units, (g + 1) * a.upg))
                for k in range(kt):
                    for i in range(4):
                        h = 4 * g + i
                        u, half = h // hpu, (k if hpu == 1 else h % hpu)
                        last = nc.tensor.matmul(o_bank[g // 2][32 * i:32 * i + dh + 1, g % 2 * sq:(g % 2 + 1) * sq],
                                                v[b.parity][0:kp, k, h, :], probs[u % a.ring][0:kp, half * sq:(half + 1) * sq],
                                                start=(k == 0), stop=(k == kt - 1))
                last.then_inc(pv_done, 1)

            def step(new, front, attend, end):
                for kind, g in a.plan:
                    if kind == "e" and attend is not None:
                        scores_t(attend, g)
                    elif kind == "pv" and attend is not None:
                        times_v(attend, g)
                    elif kind == "x" and new is not None:
                        turn(new)
                    elif kind == "qk" and new is not None:
                        project_qk(new)
                    elif kind == "v" and front is not None:
                        project_v(front)
                    elif kind in ("q", "k") and front is not None:
                        stack(front, "qk".index(kind), g)
                    elif kind == "s" and front is not None:
                        scores(front, g)
                    elif kind == "nm" and front is not None:
                        lone_wait(pe, ready, n_const, (nm_step, front.count(4, 4)), emptied(front, "nm"))
                        bank = bank_of("nm")
                        for t in range(qt):
                            last = nc.tensor.transpose(bank[:].bitcast(BF16)[0:3 * heads, t * P:(t + 1) * P],
                                                       nm_parts[:, t, :, :].rearrange("p a h -> p (a h)"), ident_b[:])
                        last.then_inc(late, 1)
                    elif kind == "tok" and end is not None:
                        pe.wait_ge(raw_ready, end.count(2, 2))
                        for t in range(qt):
                            for g in range(heads // 4):
                                last = nc.tensor.transpose(o_bank[t][:, g * P:(g + 1) * P], o_raw[:, g, t * P:(t + 1) * P], ident_f[:])
                        last.then_inc(tok_done, 1)
                    elif kind == "ot" and end is not None:
                        pe.wait_ge(o_ready, end.count(2, 2))
                        for k in range(dk):
                            for t in range(qt):
                                last = nc.tensor.transpose(o_bank[0][:, k * sq + t * P:k * sq + (t + 1) * P],
                                                           o_norm[:, t, k * P:(k + 1) * P], ident_f[:])
                        last.then_inc(ot_done, 1)
                    elif kind == "wo" and end is not None:
                        pe.wait_ge(oT_ready, end.count(1, 1))
                        for t in range(qt):
                            for k in range(dk):
                                last = nc.tensor.matmul(o_bank[1][:, t * d:(t + 1) * d], oT[:, k, t * P:(t + 1) * P],
                                                        w_o[:, k, :], start=(k == 0), stop=(k == dk - 1))
                        last.then_inc(wo_done, 1)
                    elif kind == "x2t" and end is not None:
                        pe.wait_ge(xo_ready, end.count(2, 2))
                        for k in range(dk):
                            for t in range(qt):
                                last = nc.tensor.transpose(o_bank[1][:, k * sq + t * P:k * sq + (t + 1) * P],
                                                           xo[end.parity][:, t, k * P:(k + 1) * P], ident_f[:])
                        last.then_inc(x2t_done, 1)

            run_steps(pe, a.n, step)

        @block.scalar
        def _(act):
            nc.scalar.preload_act_table_set("natural_log_exp_and_others")
            if a.cross:
                load_blocks(act, 1)
            act.wait_ge(ready, n_const)

            def step(new, front, attend, end):
                for kind, g in a.plan:
                    if kind == "e" and attend is not None:
                        e = attend
                        act.wait_ge(st_done, e.count(units, g + 1))
                        wait(act, pv_done, e.count(4, (g - a.ring) // a.upg + 1))
                        nc.scalar.activation(probs[g % a.ring][0:kp, :], e_bank[g % 2][0:kp, :], ACT.Exp,
                                             scale=float(dh) ** -0.5).then_inc(probs_ready, 1)
                    elif kind == "raw" and end is not None:
                        act.wait_ge(pv_done, end.count(4, 4))
                        wait(act, ot_done, end.count(1, 0))
                        nc.scalar.activation(o_raw[:, 2:4, :].rearrange("p g q -> p (g q)"), o_bank[1][:], ACT.Copy).then_inc(raw_ready, 1)
                    elif kind == "x" and new is not None:
                        b = new
                        act.wait_ge(*filled(b, "x"))
                        wait(act, late, b.count(n_late, names_late.index(f"v{n_v - 1}") + 1 - n_late))
                        wait(act, early, b.count(n_early, 0))
                        nc.scalar.activation(xT[:].rearrange("p k q -> p (k q)"), bank_of("x")[:], ACT.Copy).then_inc(xT_ready, 1)
                        if a.cross:
                            act.wait_ge(*filled(b, "c"))
                            nc.scalar.activation(cT[:].rearrange("p k q -> p (k q)"), bank_of("c")[:, 0:dk * kp],
                                                 ACT.Copy).then_inc(cT_ready, 1)
                    elif kind == "part1" and new is not None:
                        b = new
                        for i, (rows, t0, n) in enumerate(a.sides):
                            act.wait_ge(qk32_ready, b.count(2, i + 1 if a.cross else 2))
                            wait(act, copies_ready, b.count(4, i - 3))
                            nc.scalar.activation(part1[0:rows, t0:t0 + n], qk32[0:rows, t0:t0 + n], ACT.Copy).then_inc(part1_ready, 1)
                    elif kind == "part2" and new is not None:
                        for i, (rows, t0, n) in enumerate(a.sides):
                            act.wait_ge(rest1_ready, new.count(2, i + 1))
                            wait(act, part3_ready, new.count(2, i - 1))
                            wait(act, copies_ready, new.count(4, i - 1))
                            nc.scalar.activation(part2[0:rows, t0:t0 + n], qk32[0:rows, t0:t0 + n], ACT.Copy).then_inc(part2_ready, 1)
                    elif kind == "k" and front is not None:
                        b = front
                        act.wait_ge(*filled(b, f"k{g}"))
                        wait(act, st_done, b.count(units, -units))
                        n = a.kheads * kt * kp
                        nc.scalar.activation(kst[b.parity][0:srows, g * a.kheads:(g + 1) * a.kheads, :],
                                             bank_of(f"k{g}")[:].bitcast(BF16)[0:srows, 0:n].rearrange("p (h k) -> p h k", k=skv),
                                             ACT.Copy).then_inc(kst_ready, 1)
                    elif kind == "nm" and front is not None:
                        b = front
                        act.wait_ge(*filled(b, "nm"))
                        wait(act, nm_loaded[1 - b.parity], (b.half + b.parity) * 48)
                        nc.scalar.activation(nmT[:], bank_of("nm")[:].bitcast(BF16)[0:3 * heads, 0:sq], ACT.Copy).then_inc(nmT_ready, 1)
                    elif kind == "ot" and end is not None:
                        act.wait_ge(ot_done, end.count(1, 1))
                        wait(act, wo_done, end.count(1, 0))
                        nc.scalar.activation(oT[:].rearrange("p k q -> p (k q)"), o_bank[0][:], ACT.Copy).then_inc(oT_ready, 1)
                    elif kind == "ln" and end is not None:
                        act.wait_ge(var_ready, end.count(1, 1))
                        wait(act, rstd_ready, end.count(1, 0))
                        nc.scalar.activation(rstd0[:], var[:], ACT.Ln).then_inc(rstd0_ready, 1)
                        act.wait_ge(rstd0_ready, end.count(2, 1))
                        nc.scalar.activation(rstd0[:], rstd0[:], ACT.Exp, scale=-0.5).then_inc(rstd0_ready, 1)
                    elif kind == "x2t" and end is not None:
                        act.wait_ge(x2t_done, end.count(1, 1))
                        nc.scalar.activation(xres[:, bass.ds(end.half, 1), :, end.parity * sq:(end.parity + 1) * sq],
                                             o_bank[1][:].rearrange("p (c k q) -> p c k q", c=1, k=dk), ACT.Copy).then_inc(x2T_ready, 1)

            run_steps(act, a.n, step)

        @block.vector
        def _(dve):
            dve.wait_ge(ready, n_const)
            dve.wait_ge(ones_set, 5 if a.cross else 4)

            for i in range(2):
                nc.vector.memset(o_bank[i][:], 0.0).then_inc(banks_set, 1)

            def step(new, front, attend, end):
                for kind, g in a.plan:
                    if kind == "raw" and end is not None:
                        dve.wait_ge(pv_done, end.count(4, 2))
                        wait(dve, ot_done, end.count(1, 0))
                        nc.vector.tensor_copy(o_raw[:, 0:2, :].rearrange("p g q -> p (g q)"), o_bank[0][:]).then_inc(raw_ready, 1)
                    elif kind == "tok" and end is not None:
                        for t in range(qt):
                            dve.wait_ge(tok_done, end.count(1, 1))
                            out = o_bank[t][:].rearrange("p (h e) -> p h e", e=32)
                            nc.vector.reciprocal(rsum[:, t, :], out[:, :, dh]).then_inc(rsum_ready, 1)
                        for t in range(qt):
                            dve.wait_ge(rsum_ready, end.count(2, t + 1))
                            out = o_bank[t][:].rearrange("p (h e) -> p h e", e=32)
                            nc.vector.tensor_tensor(o_norm[:, t, :].rearrange("p (h e) -> p h e", e=dh), out[:, :, 0:dh],
                                                    rsum[:, t, :].unsqueeze(2).broadcast_to([P, heads, dh]),
                                                    ALU.mult).then_inc(o_ready, 1)
                    elif kind == "qk" and new is not None:
                        b = new
                        for i, (rows, t0, n) in enumerate(a.sides):
                            dve.wait_ge(*filled(b, f"qk{i}"))
                            wait(dve, part3_ready, b.count(2, 0))
                            if a.cross:
                                nc.vector.tensor_tensor(qk32[0:rows, t0:t0 + n],
                                                        bank_of(f"qk{i}")[0:rows, 0:n * d].rearrange("p (t e) -> p t e", e=d),
                                                        b_qkv[0:rows, i, :].unsqueeze(1).broadcast_to([rows, n, d]),
                                                        ALU.add).then_inc(qk32_ready, 1)
                            else:
                                nc.vector.tensor_tensor(qk32[:].rearrange("p (two t) e -> p two t e", two=2)[:, :, i, :],
                                                        bank_of(f"qk{i}")[:].rearrange("p (two e) -> p two e", two=2),
                                                        b_qkv[:, 0:2, :], ALU.add).then_inc(qk32_ready, 1)
                    elif kind == "v" and front is not None:
                        b = front
                        wait(dve, pv_done, b.count(4, -4))
                        for t in range(kt):
                            dve.wait_ge(*filled(b, f"v{t}"))
                            nc.vector.tensor_tensor(v[b.parity][0:kp, t, :, 0:dh],
                                                    bank_of(f"v{t}")[0:kp, 0:d].rearrange("p (h e) -> p h e", e=dh),
                                                    b_qkv[0:kp, 2, :].rearrange("p (h e) -> p h e", e=dh),
                                                    ALU.add).then_inc(v_ready, 1)
                    elif kind in ("part1", "part2") and new is not None:
                        b = new
                        for i, (rows, t0, n) in enumerate(a.sides):
                            part = (part1 if kind == "part1" else part2)[0:rows, t0:t0 + n].rearrange("p t (h e) -> p (t h) e", e=dh)
                            to = slots[0:rows, t0:t0 + n].rearrange("p t h (s e) -> p (t h) s e", e=dh)
                            nh = n * heads
                            if kind == "part1":
                                wait(dve, late, b.count(n_late, -1))
                                dve.wait_ge(part1_ready, b.count(2, i + 1))
                                twice = to[:, :, 0:2, :] if i == 0 else to[:, :, 0:4:3, :]
                                nc.vector.tensor_copy(twice, part.unsqueeze(2).broadcast_to([rows, nh, 2, dh]))
                                nc.vector.tensor_copy(to[:, :, 2 if i == 0 else 5, :], part).then_inc(copies_ready, 1)
                            else:
                                dve.wait_ge(part2_ready, b.count(2, i + 1))
                                twice = to[:, :, 3:5, :] if i == 0 else to[:, :, 1:5:3, :]
                                nc.vector.tensor_copy(twice, part.unsqueeze(2).broadcast_to([rows, nh, 2, dh])).then_inc(copies_ready, 1)
                    elif kind == "q" and front is not None:
                        b = front
                        dve.wait_ge(*filled(b, f"q{g}"))
                        wait(dve, st_done, b.count(units, -units))
                        nc.vector.tensor_copy(qst[b.parity][0:srows, g * 4:(g + 1) * 4, :],
                                              bank_of(f"q{g}")[:].bitcast(BF16)[0:srows, :].rearrange("p (h q) -> p h q", q=sq),
                                              ).then_inc(qst_ready, 1)
                    elif kind == "s" and front is not None and mask is None:
                        b = front
                        lone_wait(dve, ready, n_const, (nm_step, b.count(4, 0)))
                        dve.wait_ge(s_done, b.count(units, g + 1))
                        nc.vector.tensor_reduce(negmax[:, g * hpu:(g + 1) * hpu, :].rearrange("p h t -> p (h t)"),
                                                s_bank[g % 2][:, 0:hpu * qt * skv].rearrange("p (a k) -> p a k", k=skv),
                                                AX.X, ALU.max, negate=True).then_inc(s_read, 1)
                    elif kind == "s" and front is not None:
                        lone_wait(dve, ready, n_const, (s_done, front.count(units, g + 1)))
                        for t in range(qt):
                            sc = s_bank[g % 2][:, t * skv:(t + 1) * skv]
                            last = nc.vector.tensor_tensor_reduce(out=sc, in0=sc, in1=mask[:, t * skv:(t + 1) * skv], scale=1.0,
                                                                  scalar=-3e38, op0=ALU.add, op1=ALU.max,
                                                                  accum_out=rowmax[:, g, t:t + 1])
                        last.then_inc(s_read, 1)
                    elif kind == "neg" and front is not None and mask is not None:
                        dve.wait_ge(s_read, front.count(units, units))
                        wait(dve, nm_step, front.count(4, 0))
                        nc.vector.tensor_scalar(negmax[:], rowmax[:], -1.0, None, ALU.mult).then_inc(neg_ready, 1)
                    elif kind == "y" and end is not None:
                        o = end
                        dve.wait_ge(wo_done, o.count(1, 1))
                        dve.wait_ge(resid_ready, o.count(1, 1))
                        wait(dve, x_stored[o.parity], o.half * 16)
                        y = xo[o.parity]
                        nc.vector.tensor_tensor(y[:].rearrange("p t e -> p (t e)"), o_bank[1][:],
                                                xres_in[o.parity][:].rearrange("p t e -> p (t e)"), ALU.add).then_inc(y_ready, 1)
                        dve.wait_ge(y_ready, o.count(1, 1))
                        for t in range(qt):
                            nc.vector.bn_stats(stats[:, t, :], y[:, t, :]).then_inc(stats_ready, 1)
                        for t in range(qt):
                            lone_wait(dve, ready, n_const, (stats_ready, o.count(2, t + 1)))
                            nc.vector.bn_aggr(mv[:, t, :], stats[:, t, :]).then_inc(mv_ready, 1)
                        dve.wait_ge(mv_ready, o.count(2, 2))
                        nc.vector.tensor_scalar(var[:], mv[:, :, 1], LN_EPS, None, ALU.add).then_inc(var_ready, 1)
                    elif kind == "xo" and end is not None:
                        o = end
                        y = xo[o.parity]
                        dve.wait_ge(rstd0_ready, o.count(2, 2))
                        nc.vector.tensor_tensor(newton[:], var[:], rstd0[:], ALU.mult).then_inc(newton_step, 1)
                        dve.wait_ge(newton_step, o.count(2, 1))
                        nc.vector.scalar_tensor_tensor(newton[:], newton[:], -0.5, rstd0[:], ALU.mult, ALU.mult).then_inc(newton_step, 1)
                        dve.wait_ge(newton_step, o.count(2, 2))
                        nc.vector.scalar_tensor_tensor(rstd[:], newton[:], 1.5, rstd0[:], ALU.add, ALU.mult).then_inc(rstd_ready, 1)
                        dve.wait_ge(rstd_ready, o.count(1, 1))
                        for t in range(qt):
                            nc.vector.tensor_scalar(y[:, t, :], y[:, t, :], mv[:, t, 0:1], rstd[:, t:t + 1],
                                                    ALU.subtract, ALU.mult).then_inc(xo_ready, 1)
                        if a.cross:
                            dve.wait_ge(xo_ready, o.count(2, 2))
                            nc.vector.tensor_reduce(x2max[:, bass.ds(o.n, 1)], y[:].rearrange("p t e -> p (t e)"),
                                                    AX.X, ALU.max, apply_absolute_value=True).then_inc(xmax_ready, 1)

            run_steps(dve, a.n, step)


def decoder_layer(nc, x, ctx_in, attn, xattn, w_inT, b_in, w_out, b_out, out, x1, x2, stages=3):
    nb, s, d = x.shape
    heads = 16
    with ExitStack() as ctx:
        def sb(name, shape, dt=F32):
            return ctx.enter_context(nc.sbuf_tensor(name, shape, dt))

        ident_f = sb("ident_f", [P, P])
        ident_b = sb("ident_b", [P, P], BF16)
        x2max = sb("x2max", [P, nb])
        first = Attention(False, nb, s, s, d, heads)
        with ExitStack() as c2:
            mask = c2.enter_context(nc.sbuf_tensor("mask", [P, 2 * s], BF16))
            made = c2.enter_context(nc.semaphore("made"))
            with nc.Block() as block:
                @block.gpsimd
                def _(pool):
                    half, n_global = 32, 4
                    n = [0]

                    def then(ins):
                        n[0] += 1
                        ins.then_inc(made, 1)
                        pool.wait_ge(made, n[0])

                    for m in (ident_f, ident_b):
                        then(nc.gpsimd.memset(m[:], 0.0))
                        then(nc.gpsimd.affine_select(out=m[:], in_=m[:], compare_op=ALU.not_equal, fill=1.0, base=0,
                                                     pattern=[[-1, P]], channel_multiplier=1))
                    mk = mask[:].rearrange("p (t k) -> p t k", t=2)
                    then(nc.gpsimd.memset(mask[:], 0.0))
                    then(nc.gpsimd.affine_select(out=mk, in_=mk, compare_op=ALU.is_ge, fill=MASKED, base=half,
                                                 pattern=[[P, 2], [-1, s]], channel_multiplier=1))
                    then(nc.gpsimd.affine_select(out=mk, in_=mk, compare_op=ALU.is_ge, fill=MASKED, base=half,
                                                 pattern=[[-P, 2], [1, s]], channel_multiplier=-1))
                    then(nc.gpsimd.memset(mk[:, :, 0:n_global], 0.0))
                    then(nc.gpsimd.memset(mk[0:n_global, 0, :], 0.0))
            attention_layer(nc, first, x, None, attn, x1, ident_f, ident_b, mask, None, None)
        xres = sb("xres", [P, nb // 2, d // P, 2 * s])
        second = Attention(True, nb, s, ctx_in.shape[1], d, heads)
        attention_layer(nc, second, x1, ctx_in, xattn, x2, ident_f, ident_b, None, xres, x2max)
        ffn_layer(nc, nb, s, d, ident_f, ident_b, xres, x2max, w_inT, b_in, w_out, b_out, x2, out)


def ffn_layer(nc, nb, s, d, ident_f, ident_b, xres, x2max, w_inT, b_in, w_out, b_out, x2, out):
    dff = w_inT.shape[0]
    dk, fj = d // P, dff // P
    tc = 512
    nchunk = nb * s // tc
    tt = tc // P
    npair = fj // 2
    with ExitStack() as ctx:
        def sb(name, shape, dt=F32):
            return ctx.enter_context(nc.sbuf_tensor(name, shape, dt))

        def sem(name):
            return ctx.enter_context(nc.semaphore(name))

        w1i = sb("w1i", [P, dk, dff], BF16)
        w2q = sb("w2q", [P, fj, d])
        b1 = sb("b1", [P, fj])
        b2 = sb("b2", [P, d])
        step1 = sb("step1", [P, fj])
        gain = sb("gain", [P, fj])
        amax = sb("amax", [P, 4])
        hmax = sb("hmax", [P, nchunk, npair])
        step2 = sb("step2", [P, fj])
        gather = sb("gather", [P, 4])

        banks = [ctx.enter_context(nc.psum_tensor(f"bank{i}_f", [P, 1024], F32)) for i in range(4)]
        loaded = sem("f_loaded")
        prep = sem("f_prep")
        turned = sem("f_turned")
        spread = sem("f_spread")

        with ExitStack() as c2:
            w1 = c2.enter_context(nc.sbuf_tensor("w1", [P, fj, d], F32))
            w1b = c2.enter_context(nc.sbuf_tensor("w1b", [P, fj, d], BF16))
            w2 = c2.enter_context(nc.sbuf_tensor("w2", [P, fj, d], F32))
            a1 = c2.enter_context(nc.sbuf_tensor("a1", [P, 2, fj], F32))
            sc = c2.enter_context(nc.sbuf_tensor("sc", [P, 2, fj], F32))
            with nc.Block() as block:
                @block.sync
                def _(sp):
                    sp.dma_start(w1[:], w_inT.rearrange("(j p) e -> p j e", p=P)).then_inc(loaded, 16)
                    sp.dma_start(w2[:], w_out.rearrange("(j p) e -> p j e", p=P)).then_inc(loaded, 16)
                    with nc.allow_non_contiguous_dma("a bias of 1024"):
                        sp.dma_start(b1[:], b_in.rearrange("(j p) -> p j", p=P)).then_inc(loaded, 16)
                    sp.dma_start(b2[:], b_out.partition_broadcast(P)).then_inc(loaded, 16)
                    sp.wait_ge(loaded, 64)

                @block.vector
                def _(dve):
                    n = [0]

                    def then(ins):
                        n[0] += 1
                        ins.then_inc(prep, 1)
                        dve.wait_ge(prep, n[0])

                    then(nc.vector.tensor_reduce(amax[:, 0:1], x2max[:], AX.X, ALU.max))
                    dve.wait_ge(loaded, 64)
                    for i, w in enumerate((w1, w2)):
                        then(nc.vector.tensor_reduce(a1[:, i, :], w[:], AX.X, ALU.max, apply_absolute_value=True))
                        then(nc.vector.tensor_scalar(a1[:, i, :], a1[:, i, :], 1e-8, None, ALU.max))
                        then(nc.vector.reciprocal(sc[:, i, :], a1[:, i, :]))
                        then(nc.vector.tensor_scalar(sc[:, i, :], sc[:, i, :], 127.0, None, ALU.mult))
                        for j in range(fj):
                            then(nc.vector.tensor_scalar(w[:, j, :], w[:, j, :], sc[:, i, j:j + 1], ROUND, ALU.mult, ALU.add))
                            then(nc.vector.tensor_scalar(w[:, j, :], w[:, j, :], ROUND, 127.0, ALU.subtract, ALU.min))
                        if i == 0:
                            then(nc.vector.tensor_scalar(w1b[:], w1[:], -128.0, None, ALU.max))
                            then(nc.vector.reciprocal(step1[:], sc[:, 0, :]))
                        else:
                            then(nc.vector.reciprocal(step2[:], sc[:, 1, :]))
                            for j in range(fj):
                                then(nc.vector.tensor_scalar(w2q[:, j, :], w2[:, j, :], -128.0, None, ALU.max))
                                then(nc.vector.tensor_scalar(w2q[:, j, :], w2q[:, j, :], step2[:, j:j + 1], None, ALU.mult))
                    dve.wait_ge(spread, 1)
                    then(nc.vector.tensor_reduce(amax[:, 1:2], banks[2][:, 0:P], AX.X, ALU.max))
                    then(nc.vector.tensor_scalar(amax[:, 1:2], amax[:, 1:2], 1e-8, None, ALU.max))
                    then(nc.vector.reciprocal(amax[:, 2:3], amax[:, 1:2]))
                    then(nc.vector.tensor_scalar(amax[:, 2:3], amax[:, 2:3], 32767.0, None, ALU.mult))
                    then(nc.vector.reciprocal(amax[:, 3:4], amax[:, 2:3]))
                    then(nc.vector.tensor_scalar(gain[:], step1[:], amax[:, 3:4], None, ALU.mult))
                    for k in range(dk):
                        dve.wait_ge(turned, k + 1)
                        then(nc.vector.tensor_copy(w1i[:, k, :], banks[k][:].bitcast(BF16)[:, 0:dff]))

                @block.tensor
                def _(pe):
                    pe.wait_ge(prep, 1)
                    nc.tensor.transpose(banks[2][:, 0:P], amax[:, 0:1].broadcast_to([P, P]), ident_f[:]).then_inc(spread, 1)
                    pe.wait_ge(prep, 1 + 4 + 2 * fj + 1)
                    for k in range(dk):
                        for j in range(fj):
                            last = nc.tensor.transpose(banks[k][:].bitcast(BF16)[:, j * P:(j + 1) * P],
                                                       w1b[:, j, k * P:(k + 1) * P], ident_b[:])
                        last.then_inc(turned, 1)

        xh = xres[:].bitcast(BF16).rearrange("p c k (two n) -> p c k two n", two=2)
        with ExitStack() as c2:
            t32 = c2.enter_context(nc.sbuf_tensor("t32", [P, dk, tc], F32))
            xi = [c2.enter_context(nc.sbuf_tensor(f"xi{i}", [P, dk, tc], F32)) for i in range(2)]
            hid = [c2.enter_context(nc.sbuf_tensor(f"hid{i}", [P, 2 * tc], F32)) for i in range(2)]
            shifted = c2.enter_context(nc.semaphore("shifted"))
            rounded = c2.enter_context(nc.semaphore("rounded"))
            high = c2.enter_context(nc.semaphore("high"))
            low = c2.enter_context(nc.semaphore("low"))
            h_done = c2.enter_context(nc.semaphore("h_done"))
            h_read = c2.enter_context(nc.semaphore("h_read"))
            g_read = c2.enter_context(nc.semaphore("g_read"))
            fin = c2.enter_context(nc.semaphore("fin"))

            def passes(engine, step):
                for c in range(2):
                    step(c, c)
                with engine.Fori(0, nchunk // 2 - 1) as i:
                    for c in range(2):
                        step(i * 2 + (2 + c), c)

            with nc.Block() as block:
                @block.vector
                def _(dve):
                    def quantize(c, p):
                        chunk = xres[:, bass.ds(c, 1), :, :]
                        wait(dve, rounded, c)
                        nc.vector.tensor_scalar(t32[:].unsqueeze(1), chunk, amax[:, 2:3], ROUND, ALU.mult, ALU.add).then_inc(shifted, 1)
                        dve.wait_ge(shifted, c + 1)
                        wait(dve, low, c - 1)
                        nc.vector.tensor_scalar(xi[p][:], t32[:], ROUND, 32767.0, ALU.subtract, ALU.min).then_inc(rounded, 1)

                    def step(c, p, ahead=True):
                        if ahead:
                            quantize(c + 1, 1 - p)
                        for j in range(npair):
                            dve.wait_ge(h_read, c * npair + (j + 1))
                            nc.vector.tensor_reduce(hmax[:, bass.ds(c, 1), j], hid[j % 2][:], AX.X, ALU.max,
                                                    apply_absolute_value=True).then_inc(g_read, 1)

                    quantize(0, 0)
                    step(0, 0)
                    step(1, 1)
                    with dve.Fori(0, nchunk // 2 - 2) as i:
                        step(i * 2 + 2, 0)
                        step(i * 2 + 3, 1)
                    step(nchunk - 2, 0)
                    step(nchunk - 1, 1, False)
                    dve.wait_ge(g_read, nchunk * npair)
                    nc.vector.tensor_reduce(gather[:, 0:1], hmax[:].rearrange("p c j -> p (c j)"), AX.X, ALU.max).then_inc(fin, 1)
                    dve.wait_ge(spread, 2)
                    nc.vector.tensor_reduce(gather[:, 1:2], banks[0][:, 0:P], AX.X, ALU.max).then_inc(fin, 1)
                    dve.wait_ge(fin, 2)
                    nc.vector.tensor_scalar(gather[:, 1:2], gather[:, 1:2], 1e-8, None, ALU.max).then_inc(fin, 1)
                    dve.wait_ge(fin, 3)
                    nc.vector.reciprocal(gather[:, 2:3], gather[:, 1:2]).then_inc(fin, 1)
                    dve.wait_ge(fin, 4)
                    nc.vector.tensor_scalar(gather[:, 2:3], gather[:, 2:3], 32767.0, None, ALU.mult).then_inc(fin, 1)
                    dve.wait_ge(fin, 5)
                    nc.vector.reciprocal(gather[:, 3:4], gather[:, 2:3]).then_inc(fin, 1)
                    dve.wait_ge(fin, 6)

                @block.gpsimd
                def _(pool):
                    def step(c, p):
                        pool.wait_ge(high, c + 1)
                        nc.gpsimd.tensor_tensor(xh[:, bass.ds(c, 1), :, 1, :],
                                                xi[p][:].unsqueeze(1), xh[:, bass.ds(c, 1), :, 0, :], ALU.subtract).then_inc(low, 1)
                    passes(pool, step)

                @block.scalar
                def _(act):
                    def split(c, p):
                        act.wait_ge(rounded, c + 1)
                        nc.scalar.activation(xh[:, bass.ds(c, 1), :, 0, :], xi[p][:].unsqueeze(1), ACT.Copy).then_inc(high, 1)

                    def step(c, p, ahead=True):
                        for j in range(npair):
                            act.wait_ge(h_done, c * npair + (j + 1))
                            wait(act, g_read, c * npair + (j - 1))
                            for i in range(2):
                                ins = nc.scalar.activation(hid[j % 2][:, i * tc:(i + 1) * tc], banks[j][:, i * tc:(i + 1) * tc], ACT.Gelu,
                                                           bias=b1[:, 2 * j + i:2 * j + i + 1], scale=gain[:, 2 * j + i:2 * j + i + 1])
                            ins.then_inc(h_read, 1)
                            if j == 0 and ahead:
                                split(c + 1, 1 - p)

                    split(0, 0)
                    step(0, 0)
                    step(1, 1)
                    with act.Fori(0, nchunk // 2 - 2) as i:
                        step(i * 2 + 2, 0)
                        step(i * 2 + 3, 1)
                    step(nchunk - 2, 0)
                    step(nchunk - 1, 1, False)

                @block.tensor
                def _(pe):
                    def step(c, p):
                        pe.wait_ge(low, c + 1)
                        for j in range(npair):
                            wait(pe, h_read, c * npair + (j + 1 - npair))
                            for i in range(2):
                                col = (2 * j + i) * P
                                for k in range(dk):
                                    for part in range(2):
                                        last = nc.tensor.matmul(banks[j][:, i * tc:(i + 1) * tc], w1i[:, k, col:col + P],
                                                                xh[:, bass.ds(c, 1), k, part, :], start=(k + part == 0),
                                                                stop=(k == dk - 1 and part == 1))
                            last.then_inc(h_done, 1)
                    passes(pe, step)
                    pe.wait_ge(fin, 1)
                    nc.tensor.transpose(banks[0][:, 0:P], gather[:, 0:1].broadcast_to([P, P]), ident_f[:]).then_inc(spread, 1)

        with ExitStack() as c2:
            def sb2(name, shape, dt=F32):
                return c2.enter_context(nc.sbuf_tensor(name, shape, dt))

            def sem2(name):
                return c2.enter_context(nc.semaphore(name))

            hid = [sb2(f"g{i}", [P, 2, tc]) for i in range(2)]
            h32 = [sb2(f"h32_{i}", [P, 2, tc]) for i in range(2)]
            hq = [sb2(f"hq{i}", [P, 2, tc]) for i in range(2)]
            xr = [sb2(f"xr{i}", [P, tt, d]) for i in range(2)]
            xb = [sb2(f"xrb{i}", [P, tt, d]) for i in range(2)]
            y = sb2("fy", [P, tt, d])
            stats = sb2("fstats", [P, tt, 6])
            mv = sb2("fmv", [P, tt, 2])
            rstd = sb2("frstd", [P, tt])
            var = sb2("fvar", [P, tt])
            bits = sb2("fbits", [P, tt], I32)
            newton = sb2("fnewton", [P, tt])
            xo = [sb2(f"fxo{i}", [P, tt, d]) for i in range(2)]
            h_done, h_read = sem2("h_done2"), sem2("h_read2")
            shifted, rounded = sem2("shifted2"), sem2("rounded2")
            o_done, y_ready = sem2("o_done"), sem2("y_ready2")
            used = sem2("hq_used")
            stats_ready, mv_ready, rstd_ready, xo_ready = sem2("st2"), sem2("mv2"), sem2("rstd2"), sem2("xo2")
            resid = sem2("resid2")
            x_loaded = [sem2(f"xl2_{i}") for i in range(2)]
            x_stored = [sem2(f"xs2_{i}") for i in range(2)]
            x_view = x2.rearrange("b (t p) d -> (b t) p d", p=P)
            o_view = out.rearrange("b (t p) d -> (b t) p d", p=P)

            def chunks(engine, step):
                at = lambda c: Batch(c // 2, c % 2) if 0 <= c < nchunk else None
                for c in range(4):
                    step(at(c), at(c - 1))
                with engine.Fori(0, nchunk // 2 - 2) as i:
                    step(Batch(i + 2, 0), Batch(i + 1, 1))
                    step(Batch(i + 2, 1), Batch(i + 2, 0))
                step(None, at(nchunk - 1))

            with nc.Block() as block:
                @block.sync
                def _(sp):
                    def step(c, before):
                        if c is not None:
                            lone_wait(sp, loaded, 64, (resid, c.count(1, -1)))
                            sp.dma_start(xr[c.parity][:], x_view[bass.ds(c.n * tt, tt)].rearrange("t p d -> p t d")).then_inc(x_loaded[c.parity], 16)
                        if before is not None:
                            lone_wait(sp, loaded, 64, (xo_ready, before.count(tt, tt)))
                            sp.dma_start(o_view[bass.ds(before.n * tt, tt)].rearrange("t p d -> p t d"), xo[before.parity][:]).then_inc(x_stored[before.parity], 16)
                    chunks(sp, step)
                    for i in range(2):
                        sp.wait_ge(x_stored[i], 16 * (nchunk // 2))

                @block.gpsimd
                def _(pool):
                    def step(c, before):
                        if c is None:
                            return
                        pool.wait_ge(x_loaded[c.parity], (c.half + 1) * 16)
                        wait(pool, y_ready, c.count(tt, -tt))
                        nc.gpsimd.tensor_tensor(xb[c.parity][:], xr[c.parity][:], b2[:].unsqueeze(1).broadcast_to([P, tt, d]),
                                                ALU.add).then_inc(resid, 1)
                    chunks(pool, step)

                @block.tensor
                def _(pe):
                    def hidden(c, j):
                        wait(pe, h_read, c.count(npair, j - 1))
                        for i in range(2):
                            col = (2 * j + i) * P
                            for k in range(dk):
                                for part in range(2):
                                    last = nc.tensor.matmul(banks[j % 2][:, i * tc:(i + 1) * tc], w1i[:, k, col:col + P],
                                                            xh[:, bass.ds(c.n, 1), k, part, :], start=(k + part == 0),
                                                            stop=(k == dk - 1 and part == 1))
                        last.then_inc(h_done, 1)

                    def output(c, j):
                        if j == 0:
                            wait(pe, y_ready, c.count(tt, -tt))
                        pe.wait_ge(rounded, c.count(npair, j + 1))
                        for i in range(2):
                            for t in range(tt):
                                last = nc.tensor.matmul(banks[2 + c.parity][:, t * d:(t + 1) * d], hq[j % 2][:, i, t * P:(t + 1) * P],
                                                        w2q[:, 2 * j + i, :], start=(j + i == 0 and t % 2 == 0),
                                                        stop=(j == npair - 1 and i == 1), skip_group_check=True)
                        last.then_inc(used, 1)

                    def step(c, before):
                        for j in range(npair):
                            if c is not None:
                                hidden(c, j)
                            if j == 0 and before is not None:
                                output(before, npair - 1)
                            elif j > 0 and c is not None:
                                output(c, j - 1)
                    chunks(pe, step)

                @block.scalar
                def _(act):
                    def step(c, before):
                        if c is None:
                            return
                        for j in range(npair):
                            act.wait_ge(h_done, c.count(npair, j + 1))
                            wait(act, shifted, c.count(npair, j - 1))
                            for i in range(2):
                                ins = nc.scalar.activation(hid[j % 2][:, i, :], banks[j % 2][:, i * tc:(i + 1) * tc], ACT.Gelu,
                                                           bias=b1[:, 2 * j + i:2 * j + i + 1], scale=gain[:, 2 * j + i:2 * j + i + 1])
                            ins.then_inc(h_read, 1)
                    chunks(act, step)

                @block.vector
                def _(dve):
                    def finish(c):
                        dve.wait_ge(used, c.count(npair, npair))
                        dve.wait_ge(resid, c.count(1, 1))
                        for t in range(tt):
                            nc.vector.scalar_tensor_tensor(y[:, t, :], banks[2 + c.parity][:, t * d:(t + 1) * d], gather[:, 3:4],
                                                           xb[c.parity][:, t, :], ALU.mult, ALU.add).then_inc(y_ready, 1)
                        for t in range(tt):
                            dve.wait_ge(y_ready, c.count(tt, t + 1))
                            nc.vector.bn_stats(stats[:, t, :], y[:, t, :]).then_inc(stats_ready, 1)
                        for t in range(tt):
                            lone_wait(dve, loaded, 64, (stats_ready, c.count(tt, t + 1)))
                            nc.vector.bn_aggr(mv[:, t, :], stats[:, t, :]).then_inc(mv_ready, 1)
                        dve.wait_ge(mv_ready, c.count(tt, tt))
                        nstep = 3 + 3 * NEWTON_STEPS

                        def then(k, ins):
                            ins.then_inc(rstd_ready, 1)
                            dve.wait_ge(rstd_ready, c.count(nstep, k))

                        then(1, nc.vector.tensor_scalar(var[:], mv[:, :, 1], LN_EPS, None, ALU.add))
                        then(2, nc.vector.tensor_scalar(bits[:], var[:].bitcast(I32), 1, None, ALU.logical_shift_right))
                        then(3, nc.vector.tensor_scalar(rstd[:].bitcast(I32), bits[:], -1.0, float(0x5F3759DF), ALU.mult, ALU.add))
                        for k in range(NEWTON_STEPS):
                            then(4 + 3 * k, nc.vector.tensor_tensor(newton[:], var[:], rstd[:], ALU.mult))
                            then(5 + 3 * k, nc.vector.scalar_tensor_tensor(newton[:], newton[:], -0.5, rstd[:], ALU.mult, ALU.mult))
                            then(6 + 3 * k, nc.vector.scalar_tensor_tensor(rstd[:], newton[:], 1.5, rstd[:], ALU.add, ALU.mult))
                        wait(dve, x_stored[c.parity], c.half * 16)
                        for t in range(tt):
                            nc.vector.tensor_scalar(xo[c.parity][:, t, :], y[:, t, :], mv[:, t, 0:1], rstd[:, t:t + 1],
                                                    ALU.subtract, ALU.mult).then_inc(xo_ready, 1)

                    def step(c, before):
                        if c is not None:
                            for j in range(npair):
                                dve.wait_ge(h_read, c.count(npair, j + 1))
                                wait(dve, rounded, c.count(npair, j - 1))
                                nc.vector.tensor_scalar(h32[j % 2][:], hid[j % 2][:], gather[:, 2:3], ROUND, ALU.mult, ALU.add).then_inc(shifted, 1)
                                dve.wait_ge(shifted, c.count(npair, j + 1))
                                wait(dve, used, c.count(npair, j - 1))
                                nc.vector.tensor_scalar(hq[j % 2][:], h32[j % 2][:], ROUND, 32767.0, ALU.subtract, ALU.min).then_inc(rounded, 1)
                                if j == 1 and before is not None:
                                    finish(before)
                        elif before is not None:
                            finish(before)
                    chunks(dve, step)


_INS = ["x", "ctx_1024", "L0_attn_Wq", "L0_attn_bq", "L0_attn_Wk", "L0_attn_bk", "L0_attn_Wv", "L0_attn_bv",
        "L0_attn_Wo", "L0_attn_bo", "L0_xattn_wq", "L0_xattn_bq", "L0_xattn_wk", "L0_xattn_bk", "L0_xattn_wv",
        "L0_xattn_bv", "L0_xattn_wo", "L0_xattn_bo", "L0_ffn_W_in", "L0_ffn_b_in", "L0_ffn_W_out", "L0_ffn_b_out"]
_SWAPPED = {"L0_attn_Wq", "L0_attn_Wk", "L0_attn_Wv", "L0_attn_Wo", "L0_xattn_wq", "L0_xattn_wk", "L0_xattn_wv",
            "L0_xattn_wo", "L0_ffn_W_in"}
_FLAT = {"L0_xattn_bq", "L0_xattn_bk", "L0_xattn_bv"}


def kernel(**inputs):
    import numpy as np
    import concourse.bacc as bacc
    from concourse.bass_utils import run_bass_kernel_spmd

    nc = bacc.Bacc("TRN2", target_bir_lowering=False, num_devices=1)
    arrays, t = {}, {}
    for name in _INS:
        a = np.asarray(inputs[name])
        if name in _SWAPPED:
            a = np.swapaxes(a, -1, -2)
        if name in _FLAT:
            a = a.reshape(-1)
        a = np.ascontiguousarray(a)
        arrays[f"in_{name}"] = a
        t[name] = nc.dram_tensor(f"in_{name}", a.shape, mybir.dt.from_np(a.dtype), kind="ExternalInput").ap()
    shape = inputs["x"].shape
    out = nc.dram_tensor("out_0", shape, F32, kind="ExternalOutput").ap()
    x1 = nc.dram_tensor("x1_scratch", shape, F32, kind="Internal").ap()
    x2 = nc.dram_tensor("x2_scratch", shape, F32, kind="Internal").ap()
    attn = tuple(t[f"L0_attn_{n}"] for n in ("Wq", "Wk", "Wv", "Wo", "bq", "bk", "bv", "bo"))
    xattn = tuple(t[f"L0_xattn_{n}"] for n in ("wq", "wk", "wv", "wo", "bq", "bk", "bv", "bo"))
    decoder_layer(nc, t["x"], t["ctx_1024"], attn, xattn, t["L0_ffn_W_in"], t["L0_ffn_b_in"], t["L0_ffn_W_out"],
                  t["L0_ffn_b_out"], out, x1, x2)
    r = run_bass_kernel_spmd(nc, [arrays], core_ids=[0])
    return r.results[0]["out_0"]
```
